# Optimizing a Trainium2 kernel written in Bass

```python
import numpy as np
import jax
import jax.numpy as jnp

def _softmax(x, axis=-1):
    return jax.nn.softmax(x, axis=axis)

def _gelu(x):
    return jax.nn.gelu(x, approximate=True)

def _silu(x):
    return jax.nn.silu(x)

def _sigmoid(x):
    return jax.nn.sigmoid(x)

def _layernorm(x, axis=-1, eps=1e-05):
    m = jnp.mean(x, axis=axis, keepdims=True)
    v = jnp.var(x, axis=axis, keepdims=True)
    return (x - m) / jnp.sqrt(v + eps)

def _scatter_add(tgt, idx, src, axis=0):
    return tgt.at[idx].add(src)

def _segment_sum(src, seg, n):
    return jax.ops.segment_sum(src, seg, n)
kernel_name = 'mk_prb_d1_jaxref_r8_bbc253'

def setup_inputs(seed: int=0):
    np.random.seed(seed)
    _w = jnp.asarray

    def _L0_attn_setup():
        import math
        import jax, jax.numpy as jnp
        import numpy as np
        B, T, C = (2, 256, 256)
        H, G = (16, 4)
        D = C // H
        KV = G * D
        SOFT_CAP = 50.0
        EPS = 1e-06

        def _rmsnorm(x, w):
            rms = jnp.linalg.norm(x, axis=-1, keepdims=True) / math.sqrt(x.shape[-1])
            return w * (x / (rms + EPS))

        def _rotary_tables(seq_len, dim):
            inv_freq = 1.0 / 10000.0 ** (jnp.arange(0, dim, 2, dtype=jnp.float32) / dim)
            t = jnp.arange(seq_len, dtype=jnp.float32)
            freqs = jnp.outer(t, inv_freq)
            return (jnp.cos(freqs), jnp.sin(freqs))

        def _apply_rope(x, cos, sin):
            d = x.shape[-1] // 2
            x1, x2 = (x[..., :d], x[..., d:])
            c = cos[None, :, None, :]
            s = sin[None, :, None, :]
            return jnp.concatenate([x1 * c + x2 * s, -x1 * s + x2 * c], axis=-1)
        key = jax.random.key(seed)
        ks = jax.random.split(key, 5)
        s = 1.0 / math.sqrt(C)
        return {'x': jax.random.normal(ks[0], (B, T, C), jnp.float32), 'Wq': jax.random.normal(ks[1], (C, C), jnp.float32) * s, 'Wk': jax.random.normal(ks[2], (KV, C), jnp.float32) * s, 'Wv': jax.random.normal(ks[3], (KV, C), jnp.float32) * s, 'Wo': jax.random.normal(ks[4], (C, C), jnp.float32) * s, 'bo': jnp.zeros((C,), jnp.float32), 'q_norm_w': jnp.ones((D,), jnp.float32), 'k_norm_w': jnp.ones((D,), jnp.float32)}
    _L0_attn_in = _L0_attn_setup()

    def _L0_ffn_setup():
        import jax, jax.numpy as jnp
        import numpy as np
        D_MODEL = 256
        NUM_TILES = 64
        D_SLICE = D_MODEL // NUM_TILES
        TILES_PER_CLUSTER = 8
        NUM_CLUSTERS = NUM_TILES // TILES_PER_CLUSTER
        GRID = 16
        LN_EPS = 1e-05
        DIMS = (np.arange(NUM_TILES)[:, None] * D_SLICE + np.arange(D_SLICE)[None, :]) % D_MODEL
        DIMS = jnp.asarray(DIMS, dtype=jnp.int32)

        def _forward(x, ln_gamma, ln_beta, spline_bases, spline_slopes, output_scale):
            B, S, D = x.shape
            N = B * S
            mu = jnp.mean(x, axis=-1, keepdims=True)
            var = jnp.mean(jnp.square(x - mu), axis=-1, keepdims=True)
            xn = (x - mu) * jax.lax.rsqrt(var + LN_EPS) * ln_gamma + ln_beta
            xf = xn.reshape(N, D)
            slope_sign = jnp.sign(jnp.mean(spline_slopes, axis=-1))
            tile_sigs = jnp.zeros((NUM_TILES, D), dtype=x.dtype)
            tile_sigs = tile_sigs.at[jnp.arange(NUM_TILES)[:, None], DIMS].set(slope_sign)
            cluster_sigs = jnp.sign(tile_sigs.reshape(NUM_CLUSTERS, TILES_PER_CLUSTER, D).mean(axis=1))
            cluster_assign = jnp.arange(NUM_TILES, dtype=jnp.int32) // TILES_PER_CLUSTER
            input_sigs = jnp.sign(xf)
            cluster_scores = input_sigs @ cluster_sigs.T
            best_cluster = jnp.argmax(cluster_scores, axis=-1)
            tile_scores = input_sigs @ tile_sigs.T
            in_cluster = cluster_assign[None, :] == best_cluster[:, None]
            tile_idx = jnp.argmax(jnp.where(in_cluster, tile_scores, -jnp.inf), axis=-1)
            tok_dims = DIMS[tile_idx]
            x_slice = jnp.take_along_axis(xf, tok_dims, axis=1)
            tok_min = x_slice.min(axis=1)
            tok_max = x_slice.max(axis=1)
            onehot = tile_idx[None, :] == jnp.arange(NUM_TILES)[:, None]
            tile_min = jnp.where(onehot, tok_min[None, :], jnp.inf).min(axis=1)
            tile_max = jnp.where(onehot, tok_max[None, :], -jnp.inf).max(axis=1)
            mn = tile_min[tile_idx][:, None]
            mx = tile_max[tile_idx][:, None]
            u = jnp.clip((x_slice - mn) / (mx - mn + 1e-08), 0.0, 1.0 - 1e-06)
            gi = jnp.clip((u * GRID).astype(jnp.int32), 0, GRID - 1)
            j = jnp.arange(D_SLICE)[None, :]
            b = spline_bases[tile_idx[:, None], j, gi]
            s = spline_slopes[tile_idx[:, None], j, gi]
            x_local = (u - gi.astype(u.dtype) / GRID) * GRID
            delta = (b + s * x_local) * output_scale[tile_idx][:, None]
            out = jnp.zeros_like(xf).at[jnp.arange(N)[:, None], tok_dims].set(delta)
            return x + out.reshape(B, S, D)
        key = jax.random.key(seed)
        k1, k2, k3, k4, k5, k6 = jax.random.split(key, 6)
        x = jax.random.normal(k1, (4, 512, D_MODEL), dtype=jnp.float32)
        ln_gamma = 1.0 + 0.1 * jax.random.normal(k2, (D_MODEL,), dtype=jnp.float32)
        ln_beta = 0.1 * jax.random.normal(k3, (D_MODEL,), dtype=jnp.float32)
        spline_bases = 0.1 * jax.random.normal(k4, (NUM_TILES, D_SLICE, GRID), dtype=jnp.float32)
        spline_slopes = 0.1 + 0.1 * jax.random.normal(k5, (NUM_TILES, D_SLICE, GRID), dtype=jnp.float32)
        output_scale = 1.0 + 0.1 * jax.random.normal(k6, (NUM_TILES,), dtype=jnp.float32)
        return {'x': x, 'ln_gamma': ln_gamma, 'ln_beta': ln_beta, 'spline_bases': spline_bases, 'spline_slopes': spline_slopes, 'output_scale': output_scale}
    _L0_ffn_in = _L0_ffn_setup()
    _d = {'L0_attn_x': _L0_attn_in['x'], 'L0_attn_Wq': _L0_attn_in['Wq'], 'L0_attn_Wk': _L0_attn_in['Wk'], 'L0_attn_Wv': _L0_attn_in['Wv'], 'L0_attn_Wo': _L0_attn_in['Wo'], 'L0_attn_bo': _L0_attn_in['bo'], 'L0_attn_q_norm_w': _L0_attn_in['q_norm_w'], 'L0_attn_k_norm_w': _L0_attn_in['k_norm_w'], 'L0_ffn_ln_gamma': _L0_ffn_in['ln_gamma'], 'L0_ffn_ln_beta': _L0_ffn_in['ln_beta'], 'L0_ffn_spline_bases': _L0_ffn_in['spline_bases'], 'L0_ffn_spline_slopes': _L0_ffn_in['spline_slopes'], 'L0_ffn_output_scale': _L0_ffn_in['output_scale']}
    _x0 = _d['L0_attn_x']
    _d['L0_attn_x'] = jax.random.normal(jax.random.fold_in(jax.random.key(seed), 1), (2, 1024, 256), dtype=_x0.dtype)
    del _x0
    return _d

def reference(L0_attn_x, L0_attn_Wq, L0_attn_Wk, L0_attn_Wv, L0_attn_Wo, L0_attn_bo, L0_attn_q_norm_w, L0_attn_k_norm_w, L0_ffn_ln_gamma, L0_ffn_ln_beta, L0_ffn_spline_bases, L0_ffn_spline_slopes, L0_ffn_output_scale):

    def _L0_attn_ref(x, Wq, Wk, Wv, Wo, bo, q_norm_w, k_norm_w):
        import math
        import jax, jax.numpy as jnp
        import numpy as np
        B, T, C = (2, 256, 256)
        H, G = (16, 4)
        D = C // H
        KV = G * D
        SOFT_CAP = 50.0
        EPS = 1e-06

        def _rmsnorm(x, w):
            rms = jnp.linalg.norm(x, axis=-1, keepdims=True) / math.sqrt(x.shape[-1])
            return w * (x / (rms + EPS))

        def _rotary_tables(seq_len, dim):
            inv_freq = 1.0 / 10000.0 ** (jnp.arange(0, dim, 2, dtype=jnp.float32) / dim)
            t = jnp.arange(seq_len, dtype=jnp.float32)
            freqs = jnp.outer(t, inv_freq)
            return (jnp.cos(freqs), jnp.sin(freqs))

        def _apply_rope(x, cos, sin):
            d = x.shape[-1] // 2
            x1, x2 = (x[..., :d], x[..., d:])
            c = cos[None, :, None, :]
            s = sin[None, :, None, :]
            return jnp.concatenate([x1 * c + x2 * s, -x1 * s + x2 * c], axis=-1)
        b, t, c = x.shape
        q = (x @ Wq.T).reshape(b, t, H, D)
        k = (x @ Wk.T).reshape(b, t, G, D)
        v = (x @ Wv.T).reshape(b, t, G, D)
        cos, sin = _rotary_tables(t, D)
        q = _apply_rope(_rmsnorm(q, q_norm_w), cos, sin)
        k = _apply_rope(_rmsnorm(k, k_norm_w), cos, sin)
        q = q.transpose(0, 2, 1, 3)
        k = jnp.repeat(k.transpose(0, 2, 1, 3), H // G, axis=1)
        v = jnp.repeat(v.transpose(0, 2, 1, 3), H // G, axis=1)
        att = jnp.einsum('bhqd,bhkd->bhqk', q, k) / math.sqrt(D)
        causal = jnp.tril(jnp.ones((t, t), bool))
        att = jnp.where(causal[None, None], att, -jnp.inf)
        att = SOFT_CAP * jnp.tanh(att / SOFT_CAP)
        att = jax.nn.softmax(att, axis=-1)
        y = jnp.einsum('bhqk,bhkd->bhqd', att, v)
        y = y.transpose(0, 2, 1, 3).reshape(b, t, c)
        return y @ Wo.T + bo

    def _L0_ffn_ref(x, ln_gamma, ln_beta, spline_bases, spline_slopes, output_scale):
        import jax, jax.numpy as jnp
        import numpy as np
        D_MODEL = 256
        NUM_TILES = 64
        D_SLICE = D_MODEL // NUM_TILES
        TILES_PER_CLUSTER = 8
        NUM_CLUSTERS = NUM_TILES // TILES_PER_CLUSTER
        GRID = 16
        LN_EPS = 1e-05
        DIMS = (np.arange(NUM_TILES)[:, None] * D_SLICE + np.arange(D_SLICE)[None, :]) % D_MODEL
        DIMS = jnp.asarray(DIMS, dtype=jnp.int32)

        def _forward(x, ln_gamma, ln_beta, spline_bases, spline_slopes, output_scale):
            B, S, D = x.shape
            N = B * S
            mu = jnp.mean(x, axis=-1, keepdims=True)
            var = jnp.mean(jnp.square(x - mu), axis=-1, keepdims=True)
            xn = (x - mu) * jax.lax.rsqrt(var + LN_EPS) * ln_gamma + ln_beta
            xf = xn.reshape(N, D)
            slope_sign = jnp.sign(jnp.mean(spline_slopes, axis=-1))
            tile_sigs = jnp.zeros((NUM_TILES, D), dtype=x.dtype)
            tile_sigs = tile_sigs.at[jnp.arange(NUM_TILES)[:, None], DIMS].set(slope_sign)
            cluster_sigs = jnp.sign(tile_sigs.reshape(NUM_CLUSTERS, TILES_PER_CLUSTER, D).mean(axis=1))
            cluster_assign = jnp.arange(NUM_TILES, dtype=jnp.int32) // TILES_PER_CLUSTER
            input_sigs = jnp.sign(xf)
            cluster_scores = input_sigs @ cluster_sigs.T
            best_cluster = jnp.argmax(cluster_scores, axis=-1)
            tile_scores = input_sigs @ tile_sigs.T
            in_cluster = cluster_assign[None, :] == best_cluster[:, None]
            tile_idx = jnp.argmax(jnp.where(in_cluster, tile_scores, -jnp.inf), axis=-1)
            tok_dims = DIMS[tile_idx]
            x_slice = jnp.take_along_axis(xf, tok_dims, axis=1)
            tok_min = x_slice.min(axis=1)
            tok_max = x_slice.max(axis=1)
            onehot = tile_idx[None, :] == jnp.arange(NUM_TILES)[:, None]
            tile_min = jnp.where(onehot, tok_min[None, :], jnp.inf).min(axis=1)
            tile_max = jnp.where(onehot, tok_max[None, :], -jnp.inf).max(axis=1)
            mn = tile_min[tile_idx][:, None]
            mx = tile_max[tile_idx][:, None]
            u = jnp.clip((x_slice - mn) / (mx - mn + 1e-08), 0.0, 1.0 - 1e-06)
            gi = jnp.clip((u * GRID).astype(jnp.int32), 0, GRID - 1)
            j = jnp.arange(D_SLICE)[None, :]
            b = spline_bases[tile_idx[:, None], j, gi]
            s = spline_slopes[tile_idx[:, None], j, gi]
            x_local = (u - gi.astype(u.dtype) / GRID) * GRID
            delta = (b + s * x_local) * output_scale[tile_idx][:, None]
            out = jnp.zeros_like(xf).at[jnp.arange(N)[:, None], tok_dims].set(delta)
            return x + out.reshape(B, S, D)
        return _forward(x, ln_gamma, ln_beta, spline_bases, spline_slopes, output_scale)
    x = L0_attn_x
    xn = _layernorm(x, axis=-1)
    x = x + _L0_attn_ref(xn, L0_attn_Wq, L0_attn_Wk, L0_attn_Wv, L0_attn_Wo, L0_attn_bo, L0_attn_q_norm_w, L0_attn_k_norm_w) + _L0_ffn_ref(xn, L0_ffn_ln_gamma, L0_ffn_ln_beta, L0_ffn_spline_bases, L0_ffn_spline_slopes, L0_ffn_output_scale)
    return x

_drawn_inputs = setup_inputs


def setup_inputs(seed=0):
    import zlib

    import numpy as np

    out = dict(_drawn_inputs(seed))
    spreads = {'L0_attn_bo': (0.0, 0.1), 'L0_attn_q_norm_w': (1.0, 0.6), 'L0_attn_k_norm_w': (1.0, 0.6)}
    factors = {'L0_ffn_ln_gamma': 8.0,
     'L0_ffn_ln_beta': 7.792,
     'L0_ffn_spline_bases': 8.0,
     'L0_ffn_spline_slopes': 8.0,
     'L0_ffn_output_scale': 8.0}
    for name, (base, spread) in spreads.items():
        noise = np.random.default_rng([zlib.crc32(name.encode()), seed]).standard_normal(out[name].shape)
        drawn = base * np.exp(spread * noise) if base else spread * noise
        out[name] = jnp.asarray(drawn.astype(out[name].dtype))
    for name, factor in factors.items():
        out[name] = (out[name] * factor).astype(out[name].dtype)
    return out
```

```python
from contextlib import ExitStack

import concourse.bass as bass
from concourse import mybir
import numpy as np

P = 128
B, T, C = 2, 1024, 256
NTOK = B * T
NT = NTOK // P
TB = T // P
H, G = 16, 4
D = C // H
R = H // G
HG = H + G
SLOTS = P // D
QKW = (H + G) * D
PROJ = QKW + G * D
VW = 32
SOFT_CAP = 50.0
MASKED = float(np.exp(np.float64(-SOFT_CAP)))
SCORE_SCALE = 1.0 / (np.sqrt(D) * SOFT_CAP)
RMS_EPS = 1e-6
LN_EPS = 1e-5
TILES, SLICE, GRID, CLUSTERS = 64, 4, 16, 8
PER = TILES // CLUSTERS
FG = 4
NF = NT // FG
BIG = 3.0e38
UMAX = float(np.float32(1.0 - 1e-6))
RSQRT_MAGIC = 1597463007.0
PRING = 4
ORING = 4

UNITS = [(s, kb) for s in range(NT) for kb in range(s % TB + 1)]
NU = len(UNITS)
LAST = [max(u for u, (s, _) in enumerate(UNITS) if s == t) for t in range(NT)]

PLAN = {
    -1: [("norm", 0, 1), ("turn", 0), ("project", 0), ("rope", 0, 1)],
    0: [("norm", 1, 1), ("turn", 1), ("project", 1), ("rope", 1, 1)],
    1: [("norm", 2, 2), ("turn", 2), ("project", 2)],
    2: [("turn", 3), ("project", 3), ("rope", 2, 2)],
    3: [("norm", 4, 2), ("turn", 4), ("project", 4)],
    5: [("turn", 5), ("project", 5), ("rope", 4, 2)],
    6: [("norm", 6, 2), ("turn", 6), ("project", 6)],
    8: [("turn", 7), ("project", 7), ("rope", 6, 2)],
    9: [("suffix", 0)],
    11: [("norm", 8, 2), ("ffn_norm", 0)],
    14: [("turn", 8)], 15: [("project", 8)], 16: [("turn", 9)], 17: [("project", 9), ("rope", 8, 2)],
    19: [("ffn_route", 0)],
    21: [("norm", 10, 2), ("turn", 10)], 22: [("project", 10)], 23: [("turn", 11)],
    24: [("project", 11), ("rope", 10, 2)],
    25: [("ffn_norm", 1)],
    27: [("norm", 12, 2), ("turn", 12)], 28: [("project", 12)], 29: [("turn", 13)],
    30: [("project", 13), ("rope", 12, 2)],
    32: [("ffn_route", 1)],
    34: [("norm", 14, 2), ("turn", 14)], 35: [("project", 14)], 36: [("turn", 15)],
    37: [("project", 15), ("rope", 14, 2)],
    38: [("suffix", 1), ("ffn_norm", 2)], 41: [("ffn_norm", 3)],
    43: [("ffn_route", 2)], 46: [("ffn_route", 3)],
    48: [("extremes",)], 49: [("extremes_row",)], 50: [("ffn_grid",)],
}


def add(u, *task):
    PLAN.setdefault(u, []).append(task)


for _f, _u in enumerate((7, 10, 27, 39)):
    add(_u, "base", _f)

_free = 10
for _s in range(NT):
    _free = max(_free, LAST[_s] + 3)
    if _free + 2 < NU:
        for _k, _name in enumerate(("out_norm", "out_turn", "out_project")):
            add(_free + _k, _name, _s)
        _free += 2
    else:
        for _name in ("out_norm", "out_turn", "out_project"):
            add(NU + 1, _name, _s)
for _f in range(NF):
    add(53 + 4 * _f, "pick_turn", _f)
    add(54 + 4 * _f, "pick", _f)
PLAN = {u: PLAN[u] for u in sorted(PLAN)}
FRONT = ("turn", "project", "suffix")
BACK = ("out_norm", "out_turn", "out_project", "extremes", "extremes_row", "pick_turn", "pick", "signs")

V_GAMMA, V_BETA, V_BO, V_KEY, V_GRID = 0, C, 2 * C, 3 * C, 3 * C + TILES
V_ALL = 3 * C + TILES + GRID


def build(nc, x, wproj, wo, vectors, tables, wnorm, grid_rows, ident, out):
    f32, bf16, i32 = mybir.dt.float32, mybir.dt.bfloat16, mybir.dt.int32
    ALU = mybir.AluOpType
    ACT = mybir.ActivationFunctionType
    X = mybir.AxisListType.X
    ctx = ExitStack()
    with ctx:
        def sb(name, shape, dt=f32):
            return ctx.enter_context(nc.sbuf_tensor(name, shape, dt))

        def pb(name, shape, dt=f32):
            return ctx.enter_context(nc.psum_tensor(name, shape, dt))

        def sem(name):
            return ctx.enter_context(nc.semaphore(name))

        xs = sb("xs", [P, NT, C])
        xn = sb("xn", [P, NT, C])
        xf = sb("xf", [P, NT, C])
        xnT = sb("xnT", [P, 2, P])
        wproj_sb = sb("wproj_sb", [P, 2, PROJ])
        wo_sb = sb("wo_sb", [P, 2, C])
        vec = sb("vec", [P, V_ALL])
        tab = sb("tab", [P, TB, 2, 2, D])
        tab_raw = sb("tab_raw", [P, TB, 2, D])
        wn = sb("wn", [P, 2, 2, D])
        rows = sb("rows", [TILES, 2 * SLICE * GRID + 1])
        idn = sb("idn", [P, P])
        masked = sb("masked", [P, P])
        raw = sb("raw", [P, 2, QKW])
        rot = sb("rot", [P, 2, QKW])
        tmp = sb("tmp", [P, 2, QKW])
        parts = sb("parts", [P, 3, 2, QKW], bf16)
        combos = sb("combos", [P, 2, HG, SLOTS, D], bf16)
        qT = sb("qT", [P, TB, H, P], bf16)
        kT = sb("kT", [P, NT, G, P], bf16)
        val = sb("val", [P, NT, G, VW])
        suffix = sb("suffix", [P, B, TB - 1, G, D + 1])
        probs = sb("probs", [P, PRING, H, P])
        oT = sb("oT", [P, ORING, G * P])
        osum = sb("osum", [P, H, D + 1])
        oinv = sb("oinv", [P, H])
        y = sb("y", [P, C])
        yT = sb("yT", [P, 2, P])
        stats = sb("stats", [P, FG, 6])
        mv = sb("mv", [P, FG, 2])
        small = sb("small", [P, 6, 2 * HG])
        small_i = sb("small_i", [P, 2 * HG], i32)
        big = sb("big", [P, FG, C])
        tsc = sb("tsc", [P, FG, TILES])
        key = sb("key", [P, FG, TILES])
        csc = sb("csc", [P, FG * CLUSTERS])
        best = sb("best", [P, FG])
        chosen = sb("chosen", [P, NT, TILES])
        xsl = sb("xsl", [P, NT, SLICE])
        ends = sb("ends", [P, 2, FG])
        cand = sb("cand", [P, 2, FG, TILES])
        low = sb("low", [P, 2, TILES])
        lowc = sb("lowc", [P, 1])
        lowb = sb("lowb", [P, P])
        lowr = sb("lowr", [P, 2, TILES])
        tmn = sb("tmn", [P, 2, NT])
        rng = sb("rng", [P, NT])
        u16 = sb("u16", [P, NT, SLICE])
        gi = sb("gi", [P, NT, SLICE])
        hot = xf[:, 0:NT * SLICE * GRID // C].rearrange("p a (b m) -> p (a b) m", m=SLICE * GRID)
        ss = sb("ss", [P, TILES, SLICE])
        sgn = sb("sgn", [TILES, SLICE])
        sgn_ge = sb("sgn_ge", [TILES, SLICE])
        sdiag = sb("sdiag", [TILES, TILES, SLICE])
        ones = sb("ones", [TILES, P])
        chT = sb("chT", [TILES, FG, P])
        bsel = sb("bsel", [P, FG, 2, SLICE])
        delta = sb("delta", [P, FG, SLICE])

        scores = pb("scores", [P, H, P])
        oacc = pb("oacc", [P, 2, G * P])
        front = pb("front", [P, 512])
        back = pb("back", [P, 512])

        xchunks = [(0, 1), (1, 1), (2, 2), (4, 4), (8, 4), (12, 4)]
        x_in = [sem(f"x_in{i}") for i in range(len(xchunks))]
        ident_in, wproj_in, vec_in, tab_in, wn_in, wo_in, rows_in = (
            sem(n) for n in ("ident_in", "wproj_in", "vec_in", "tab_in", "wn_in", "wo_in", "rows_in"))
        const_ready = sem("const_ready")
        xn_ready = sem("xn_ready")
        front_filled, front_read = sem("front_filled"), sem("front_read")
        back_filled, back_read = sem("back_filled"), sem("back_read")
        combos_ready = sem("combos_ready")
        turned = sem("turned")
        scores_ready, tanh_done, exp_done, mask_done, pv_done = (
            sem(n) for n in ("scores_ready", "tanh_done", "exp_done", "mask_done", "pv_done"))
        oacc_read = sem("oacc_read")
        dve_chain = sem("dve_chain")
        pool_chain = sem("pool_chain")
        normed2 = sem("normed2")
        xf_ready = sem("xf_ready")
        base_ready = sem("base_ready")
        lowb_ready = sem("lowb_ready")
        signs_rhs = sem("signs_rhs")
        attn_added = sem("attn_added")
        delta_added = sem("delta_added")
        out_done = sem("out_done")

        FRONT_USES = [t for ts in PLAN.values() for t in ts if t[0] in FRONT]
        BACK_USES = [("signs",)] + [t for ts in PLAN.values() for t in ts if t[0] in BACK]
        front_use = FRONT_USES.index
        back_use = BACK_USES.index

        block = ctx.enter_context(nc.Block())

        @block.sync
        def _(sp):
            sp.dma_start(xs[:, 0:1], x[:, 0:1]).then_inc(x_in[0], 16)
            sp.dma_start(wproj_sb[:], wproj).then_inc(wproj_in, 16)
            sp.dma_start(xs[:, 1:2], x[:, 1:2]).then_inc(x_in[1], 16)
            for i in range(2, len(xchunks)):
                t0, n = xchunks[i]
                sp.dma_start(xs[:, t0:t0 + n], x[:, t0:t0 + n]).then_inc(x_in[i], 16)
            for t in range(NT):
                sp.wait_ge(combos_ready, t + 1)
                if t:
                    sp.wait_ge(turned, 32 * t)
                if t >= TB:
                    sp.wait_ge(scores_ready, LAST[t - TB] + 1)
                sp.dma_start_transpose(qT[:, t % TB], combos[:, t % 2, 0:H].rearrange("p h s d -> p (h s d)"))\
                    .then_inc(turned, 16)
                sp.wait_ge(turned, 32 * t + 16)
                sp.dma_start_transpose(kT[:, t], combos[:, t % 2, H:HG].rearrange("p h s d -> p (h s d)"))\
                    .then_inc(turned, 16)
            for t in range(NT):
                sp.wait_ge(attn_added, t + 1)
                sp.wait_ge(delta_added, t // FG + 1)
                sp.dma_start(out[:, t], xs[:, t]).then_inc(out_done, 16)
            sp.wait_ge(out_done, 16 * NT)

        @block.gpsimd
        def _(pool):
            nc.gpsimd.memset(masked[:], MASKED).then_inc(const_ready, 1)
            nc.gpsimd.memset(ones[:], 1.0).then_inc(const_ready, 1)
            nc.gpsimd.memset(val[:, :, :, D:VW], 0.0).then_inc(pool_chain, 1)
            pool.wait_ge(pool_chain, 1)
            nc.gpsimd.memset(val[:, :, :, D:D + 1], 1.0).then_inc(const_ready, 1)
            chain = [1]

            def link(ins):
                chain[0] += 1
                ins.then_inc(pool_chain, 1)
                pool.wait_ge(pool_chain, chain[0])

            def every(v0):
                return vec[:, v0:v0 + C].rearrange("p (o c) -> p o c", o=1).broadcast_to([P, FG, C])

            for u in range(-1, NU + 2):
                if u >= 0 and u < NU and UNITS[u][1] == UNITS[u][0] % TB:
                    pool.wait_ge(exp_done, u + 1)
                    pr = probs[:, u % PRING]
                    nc.gpsimd.affine_select(out=pr, in_=pr, pattern=[[0, H], [1, P]], compare_op=ALU.is_ge,
                                            fill=MASKED, base=0, channel_multiplier=-1).then_inc(mask_done, 1)
                for task in PLAN.get(u, ()):
                    if task[0] == "ffn_norm":
                        f = task[1]
                        fs = slice(FG * f, FG * f + FG)
                        pool.wait_ge(normed2, f + 1)
                        link(nc.gpsimd.tensor_tensor(xf[:, fs], xf[:, fs], every(V_GAMMA), ALU.mult))
                        nc.gpsimd.tensor_tensor(xf[:, fs], xf[:, fs], every(V_BETA), ALU.add).then_inc(xf_ready, 1)
                    elif task[0] == "base":
                        f = task[1]
                        fs = slice(FG * f, FG * f + FG)
                        if f == 0:
                            pool.wait_ge(vec_in, 16)
                        pool.wait_ge(xn_ready, FG * f + FG)
                        link(nc.gpsimd.tensor_tensor(xs[:, fs], xs[:, fs], xn[:, fs], ALU.add))
                        nc.gpsimd.tensor_tensor(xs[:, fs], xs[:, fs], every(V_BO), ALU.add).then_inc(base_ready, 1)

        @block.scalar
        def _(act):
            act.dma_start(idn[:], ident).then_inc(ident_in, 16)
            act.dma_start(wn[:], wnorm).then_inc(wn_in, 16)
            act.dma_start(tab_raw[:], tables).then_inc(tab_in, 16)
            act.dma_start(vec[:], vectors).then_inc(vec_in, 16)
            act.dma_start(rows[:], grid_rows).then_inc(rows_in, 16)
            act.dma_start(wo_sb[:], wo).then_inc(wo_in, 16)
            nc.scalar.preload_act_table(ACT.Tanh)
            for u in range(NU):
                pr = probs[:, u % PRING]
                act.wait_ge(scores_ready, u + 1)
                if u >= PRING:
                    act.wait_ge(pv_done, u - PRING + 1)
                nc.scalar.activation(pr, scores[:], ACT.Tanh, scale=SCORE_SCALE).then_inc(tanh_done, 1)
                act.wait_ge(tanh_done, u + 1)
                nc.scalar.activation(pr, pr, ACT.Exp, scale=SOFT_CAP).then_inc(exp_done, 1)

        @block.tensor
        def _(pe):
            def take_front(task):
                n = front_use(task)
                if n:
                    pe.wait_ge(front_read, n)

            def take_back(task):
                n = back_use(task)
                if n:
                    pe.wait_ge(back_read, n)

            def score(u):
                s, kb = UNITS[u]
                kt = s - s % TB + kb
                if kb == 0:
                    pe.wait_ge(turned, 32 * (s + 1))
                if u:
                    pe.wait_ge(tanh_done, u)
                for g in range(G):
                    last = nc.tensor.matmul(scores[:, R * g:R * g + R, :], kT[:, kt, g, :],
                                            qT[:, s % TB, R * g:R * g + R, :], start=True, stop=True)
                last.then_inc(scores_ready, 1)

            def value(u):
                s, kb = UNITS[u]
                kt = s - s % TB + kb
                pe.wait_ge(exp_done, u + 1)
                if kb == s % TB:
                    pe.wait_ge(mask_done, s + 1)
                if kb == 0 and s >= 2:
                    pe.wait_ge(oacc_read, s - 1)
                if u == 0:
                    pe.wait_ge(const_ready, 3)
                pe.wait_ge(front_read, front_use(("project", kt)) + 1)
                for g in range(G):
                    for r in range(R):
                        last = nc.tensor.matmul(oacc[VW * r:VW * r + VW, s % 2, P * g:P * g + P],
                                                val[:, kt, g, :], probs[:, u % PRING, R * g + r, :],
                                                start=(kb == 0 and g == 0), stop=(kb == s % TB),
                                                skip_group_check=True)
                last.then_inc(pv_done, 1)

            pe.wait_ge(signs_rhs, 1)
            pe.wait_ge(const_ready, 2)
            nc.tensor.matmul(back[:, 0:C], ones[:], sdiag[:].rearrange("k t j -> k (t j)"),
                             start=True, stop=True).then_inc(back_filled, 1)

            def do(task):
                kind = task[0]
                if kind == "turn":
                    t = task[1]
                    take_front(task)
                    pe.wait_ge(xn_ready, t + 1)
                    if t == 0:
                        pe.wait_ge(ident_in, 16)
                    for c in range(2):
                        last = nc.tensor.transpose(front[:, P * c:P * c + P], xn[:, t, P * c:P * c + P], idn[:])
                    last.then_inc(front_filled, 1)
                elif kind == "project":
                    take_front(task)
                    if task[1] == 0:
                        pe.wait_ge(wproj_in, 16)
                    for c in range(2):
                        last = nc.tensor.matmul(front[:, 0:PROJ], xnT[:, c], wproj_sb[:, c], start=(c == 0), stop=(c == 1))
                    last.then_inc(front_filled, 1)
                elif kind == "suffix":
                    b = task[1]
                    take_front(task)
                    for qt in range(TB - 1):
                        for kb in range(qt + 1, TB):
                            o = qt * G * (D + 1)
                            last = nc.tensor.matmul(front[:, o:o + G * (D + 1)].rearrange("p (g d) -> p g d", g=G),
                                                    masked[:], val[:, TB * b + kb, :, 0:D + 1],
                                                    start=(kb == qt + 1), stop=(kb == TB - 1))
                    last.then_inc(front_filled, 1)
                elif kind == "out_norm":
                    s = task[1]
                    take_back(task)
                    pe.wait_ge(oacc_read, s + 1)
                    for g in range(G):
                        last = nc.tensor.transpose(back[:, P * g:P * g + P], oT[:, s % ORING, P * g:P * g + P], idn[:])
                    last.then_inc(back_filled, 1)
                elif kind == "out_turn":
                    take_back(task)
                    for c in range(2):
                        last = nc.tensor.transpose(back[:, P * c:P * c + P], y[:, P * c:P * c + P], idn[:])
                    last.then_inc(back_filled, 1)
                elif kind == "out_project":
                    if task[1] == 0:
                        pe.wait_ge(wo_in, 16)
                    take_back(task)
                    for c in range(2):
                        last = nc.tensor.matmul(back[:, 0:C], yT[:, c], wo_sb[:, c], start=(c == 0), stop=(c == 1))
                    last.then_inc(back_filled, 1)
                elif kind == "extremes":
                    take_back(task)
                    pe.wait_ge(lowb_ready, 1)
                    nc.tensor.transpose(back[:, 0:P], low[:].rearrange("p a t -> p (a t)"), idn[:]).then_inc(back_filled, 1)
                elif kind == "extremes_row":
                    take_back(task)
                    pe.wait_ge(lowb_ready, 2)
                    nc.tensor.matmul(back[:, 0:P], lowb[:], idn[:], start=True, stop=True).then_inc(back_filled, 1)
                elif kind == "pick_turn":
                    f = task[1]
                    take_back(task)
                    for i in range(FG):
                        last = nc.tensor.transpose(back[0:TILES, P * i:P * i + P], chosen[:, FG * f + i, :], idn[:])
                    last.then_inc(back_filled, 1)
                elif kind == "pick":
                    take_back(task)
                    for i in range(FG):
                        last = nc.tensor.matmul(back[:, P * i:P * i + P], chT[:, i], rows[:, 0:P], start=True, stop=True)
                    last.then_inc(back_filled, 1)

            for u in range(-1, NU + 2):
                if 0 <= u < NU:
                    score(u)
                if u >= 2:
                    value(u - 2)
                for task in PLAN.get(u, ()):
                    do(task)

        @block.vector
        def _(dve):
            chain = [0]

            def link(ins):
                chain[0] += 1
                ins.then_inc(dve_chain, 1)
                dve.wait_ge(dve_chain, chain[0])

            V = nc.vector

            def rsqrt(v, n):
                g0, a, b = small[:, 0, 0:n], small[:, 1, 0:n], small[:, 2, 0:n]
                link(V.tensor_scalar(small_i[:, 0:n], v.bitcast(i32), 1, None, ALU.logical_shift_right))
                link(V.tensor_scalar(g0.bitcast(i32), small_i[:, 0:n], -1.0, RSQRT_MAGIC, ALU.mult, ALU.add))
                for _ in range(4):
                    link(V.scalar_tensor_tensor(a, v, -0.5, g0, ALU.mult, ALU.mult))
                    link(V.tensor_tensor(b, a, g0, ALU.mult))
                    link(V.scalar_tensor_tensor(g0, b, 1.5, g0, ALU.add, ALU.mult))
                return g0

            def layernorm(src, dst, t0, n, done):
                for i in range(n):
                    last = V.bn_stats(stats[:, i], src[:, t0 + i])
                link(last)
                for i in range(n):
                    last = V.bn_aggr(mv[:, i], stats[:, i])
                link(last)
                v = small[:, 3, 0:n]
                link(V.tensor_scalar(v, mv[:, 0:n, 1], LN_EPS, None, ALU.add))
                r = rsqrt(v, n)
                for i in range(n):
                    ins = V.tensor_scalar(dst[:, t0 + i], src[:, t0 + i], mv[:, i, 0:1], r[:, i:i + 1],
                                          ALU.subtract, ALU.mult)
                    done(i, ins)

            def rope(t0, n):
                m = n * HG
                qk = raw[:, t0 % 2:t0 % 2 + n]
                heads = qk.rearrange("p n (h d) -> p n h d", d=D)
                sq = tmp[:, 0:n]
                link(V.tensor_tensor(sq, qk, qk, ALU.mult))
                ssq = small[:, 3, 0:m]
                link(V.tensor_reduce(ssq, sq.rearrange("p n (h d) -> p (n h) d", d=D), X, ALU.add))
                mean = small[:, 4, 0:m]
                link(V.tensor_scalar(mean, ssq, 1.0 / D, None, ALU.mult))
                r = rsqrt(mean, m)
                rms = small[:, 5, 0:m]
                link(V.tensor_tensor(rms, mean, r, ALU.mult))
                link(V.tensor_scalar(rms, rms, RMS_EPS, None, ALU.add))
                link(V.reciprocal(ssq, rms))
                inv = ssq
                p0 = t0 % TB
                half = D // 2
                rv = rot[:, 0:n].rearrange("p n (h d) -> p n h d", d=D)
                tv = tmp[:, 0:n].rearrange("p n (h d) -> p n h d", d=D)
                for i in range(n):
                    for w, (h0, h1) in enumerate(((0, H), (H, HG))):
                        cos = tab[:, p0 + i, 0, w:w + 1, :].broadcast_to([P, h1 - h0, D])
                        V.tensor_tensor(rv[:, i, h0:h1], heads[:, i, h0:h1], cos, ALU.mult)
                        for lo, hi in ((0, half), (half, D)):
                            sin = tab[:, p0 + i, 1, w:w + 1, lo:hi].broadcast_to([P, h1 - h0, half])
                            last = V.tensor_tensor(tv[:, i, h0:h1, lo:hi], heads[:, i, h0:h1, D - hi:D - lo], sin, ALU.mult)
                link(last)
                link(V.tensor_tensor(rot[:, 0:n], rot[:, 0:n], tmp[:, 0:n], ALU.add))
                rall = rot[:, 0:n].rearrange("p n (h d) -> p (n h) d", d=D)
                ib = inv.rearrange("p (h o) -> p h o", o=1).broadcast_to([P, m, D])
                link(V.tensor_tensor(rall, rall, ib, ALU.mult))
                p1, p2, p3 = (parts[:, k, 0:n] for k in range(3))
                link(V.tensor_copy(p1, rot[:, 0:n]))
                link(V.tensor_tensor(rot[:, 0:n], rot[:, 0:n], p1, ALU.subtract))
                link(V.tensor_copy(p2, rot[:, 0:n]))
                link(V.tensor_tensor(p3, rot[:, 0:n], p2, ALU.subtract))
                if t0:
                    dve.wait_ge(turned, 32 * t0)
                for i in range(n):
                    c = combos[:, (t0 + i) % 2]

                    def part(k, h0, h1):
                        v = parts[:, k, i, D * h0:D * h1].rearrange("p (h o d) -> p h o d", o=1, d=D)
                        return lambda m: v.broadcast_to([P, h1 - h0, m, D])

                    V.tensor_copy(c[:, 0:H, 0:3], part(0, 0, H)(3))
                    V.tensor_copy(c[:, 0:H, 3:6], part(1, 0, H)(3))
                    V.tensor_copy(c[:, 0:H, 6:8], part(2, 0, H)(2))
                    V.tensor_copy(c[:, H:HG, 0:7:3], part(0, H, HG)(3))
                    V.tensor_copy(c[:, H:HG, 1:8:3], part(1, H, HG)(3))
                    V.tensor_copy(c[:, H:HG, 2:6:3], part(2, H, HG)(2)).then_inc(combos_ready, 1)

            def ffn_route(f):
                fs = slice(FG * f, FG * f + FG)
                dve.wait_ge(xf_ready, f + 1)
                link(V.tensor_scalar(big[:], xf[:, fs], 0.0, -1.0, ALU.is_ge, ALU.add))
                link(V.scalar_tensor_tensor(big[:], xf[:, fs], 0.0, big[:], ALU.is_gt, ALU.add))
                sb_ = ss[:].rearrange("p t j -> p (t j)").rearrange("p (o c) -> p o c", o=1).broadcast_to([P, FG, C])
                link(V.tensor_tensor(big[:], big[:], sb_, ALU.mult))
                link(V.tensor_reduce(tsc[:].rearrange("p n t -> p (n t)"), big[:].rearrange("p n (t j) -> p (n t) j", j=SLICE), X, ALU.add))
                link(V.tensor_reduce(csc[:], tsc[:].rearrange("p n (c k) -> p (n c) k", k=PER), X, ALU.add))
                kc = vec[:, V_KEY:V_KEY + TILES].rearrange("p (o t) -> p o t", o=1).broadcast_to([P, FG, TILES])
                link(V.scalar_tensor_tensor(key[:], tsc[:], float(PER), kc, ALU.mult, ALU.add))
                k3 = key[:].rearrange("p n (c k) -> p (n c) k", k=PER)
                cb = csc[:].rearrange("p (c o) -> p c o", o=1).broadcast_to([P, FG * CLUSTERS, PER])
                link(V.scalar_tensor_tensor(k3, cb, float(PER * P), k3, ALU.mult, ALU.add))
                link(V.tensor_reduce(best[:], key[:], X, ALU.max))
                bb = best[:].rearrange("p (n o) -> p n o", o=1).broadcast_to([P, FG, TILES])
                oh = chosen[:, fs]
                link(V.tensor_tensor(oh, key[:], bb, ALU.is_equal))
                ohb = oh.rearrange("p n (t o) -> p (n t) o", o=1).broadcast_to([P, FG * TILES, SLICE])
                link(V.tensor_tensor(big[:].rearrange("p n (t j) -> p (n t) j", j=SLICE),
                                     xf[:, fs].rearrange("p n (t j) -> p (n t) j", j=SLICE), ohb, ALU.mult))
                link(V.tensor_reduce(xsl[:, fs], big[:].rearrange("p n (t j) -> p n j t", j=SLICE), X, ALU.add))
                V.tensor_reduce(ends[:, 0], xsl[:, fs], X, ALU.min)
                link(V.tensor_reduce(ends[:, 1], xsl[:, fs], X, ALU.max))
                link(V.tensor_scalar(ends[:, 1], ends[:, 1], -1.0, None, ALU.mult))
                for a in range(2):
                    eb = ends[:, a].rearrange("p (n o) -> p n o", o=1).broadcast_to([P, FG, TILES])
                    last = V.tensor_tensor(cand[:, a], oh, eb, ALU.mult)
                link(V.tensor_scalar(key[:], oh, -BIG, BIG, ALU.mult, ALU.add))
                for a in range(2):
                    last = V.tensor_tensor(cand[:, a], cand[:, a], key[:], ALU.add)
                link(last)
                if f == 0:
                    for a in range(2):
                        last = V.tensor_reduce(low[:, a], cand[:, a].rearrange("p n t -> p t n"), X, ALU.min)
                    link(last)
                else:
                    for a in range(2):
                        last = V.tensor_reduce(key[:, a], cand[:, a].rearrange("p n t -> p t n"), X, ALU.min)
                    link(last)
                    ins = V.tensor_tensor(low[:], low[:], key[:, 0:2], ALU.min)
                    if f == NF - 1:
                        ins.then_inc(lowb_ready, 1)
                    else:
                        link(ins)

            def do(task):
                kind = task[0]
                if kind in FRONT:
                    dve.wait_ge(front_filled, front_use(task) + 1)
                if kind in BACK:
                    dve.wait_ge(back_filled, back_use(task) + 1)
                if kind == "norm":
                    t0, n = task[1:]
                    for i, (c0, cn) in enumerate(xchunks):
                        if t0 <= c0 < t0 + n:
                            dve.wait_ge(x_in[i], 16)
                    layernorm(xs, xn, t0, n, lambda i, ins: ins.then_inc(xn_ready, 1))
                elif kind == "turn":
                    V.tensor_copy(xnT[:].rearrange("p c t -> p (c t)"), front[:, 0:C]).then_inc(front_read, 1)
                elif kind == "project":
                    t = task[1]
                    V.tensor_copy(raw[:, t % 2], front[:, 0:QKW]).then_inc(dve_chain, 1)
                    chain[0] += 1
                    if t == 0:
                        dve.wait_ge(const_ready, 3)
                    V.tensor_copy(val[:, t, :, 0:D], front[:, QKW:PROJ].rearrange("p (g d) -> p g d", g=G)).then_inc(front_read, 1)
                    dve.wait_ge(dve_chain, chain[0])
                elif kind == "rope":
                    rope(*task[1:])
                elif kind == "suffix":
                    V.tensor_copy(suffix[:, task[1]].rearrange("p q g d -> p (q g d)"),
                                  front[:, 0:(TB - 1) * G * (D + 1)]).then_inc(front_read, 1)
                elif kind == "out_norm":
                    s = task[1]
                    b, qt = divmod(s, TB)
                    acc = back[:].rearrange("p (g r w) -> p g r w", g=G, w=VW)
                    dst = osum[:].rearrange("p (g r) d -> p g r d", g=G)
                    if qt < TB - 1:
                        if qt == 0:
                            dve.wait_ge(front_read, front_use(("suffix", b)) + 1)
                        for g in range(G):
                            sfx = suffix[:, b, qt, g:g + 1, :].broadcast_to([P, R, D + 1])
                            last = V.tensor_tensor(dst[:, g], acc[:, g, :, 0:D + 1], sfx, ALU.add)
                        link(last)
                    else:
                        link(V.tensor_copy(dst, acc[:, :, :, 0:D + 1]))
                    link(V.reciprocal(oinv[:], osum[:, :, D]))
                    ob = oinv[:].rearrange("p (h o) -> p h o", o=1).broadcast_to([P, H, D])
                    V.tensor_tensor(y[:].rearrange("p (h d) -> p h d", d=D), osum[:, :, 0:D], ob, ALU.mult).then_inc(back_read, 1)
                elif kind == "out_turn":
                    V.tensor_copy(yT[:].rearrange("p c t -> p (c t)"), back[:, 0:C]).then_inc(back_read, 1)
                elif kind == "out_project":
                    s = task[1]
                    dve.wait_ge(base_ready, s // FG + 1)
                    V.tensor_tensor(xs[:, s], xs[:, s], back[:, 0:C], ALU.add).then_inc(attn_added, 1)
                    V.engine_nop().then_inc(back_read, 1)
                elif kind == "ffn_norm":
                    f = task[1]
                    def done(i, ins):
                        if i == FG - 1:
                            ins.then_inc(normed2, 1)
                    dve.wait_ge(xn_ready, FG * f + FG)
                    layernorm(xn, xf, FG * f, FG, done)
                elif kind == "ffn_route":
                    ffn_route(task[1])
                elif kind == "extremes":
                    link(V.tensor_reduce(lowc[:], back[:, 0:P], X, ALU.min))
                    V.tensor_scalar(lowb[:], masked[:], 0.0, lowc[:], ALU.mult, ALU.add).then_inc(lowb_ready, 1)
                    dve.wait_ge(lowb_ready, 2)
                    V.engine_nop().then_inc(back_read, 1)
                elif kind == "extremes_row":
                    V.tensor_copy(lowr[:].rearrange("p a t -> p (a t)"), back[:, 0:P]).then_inc(back_read, 1)
                    dve.wait_ge(back_read, back_use(task) + 1)
                elif kind == "ffn_grid":
                    wide = big[:].rearrange("p a c -> p (a c)").rearrange("p (n t) -> p n t", n=NT)
                    for a in range(2):
                        lb = lowr[:, a:a + 1].broadcast_to([P, NT, TILES])
                        link(V.tensor_tensor(wide, chosen[:], lb, ALU.mult))
                        link(V.tensor_reduce(tmn[:, a], wide, X, ALU.add))
                    link(V.scalar_tensor_tensor(rng[:], tmn[:, 1], -1.0, tmn[:, 0], ALU.mult, ALU.subtract))
                    link(V.tensor_scalar(rng[:], rng[:], 1e-8, None, ALU.add))
                    link(V.reciprocal(rng[:], rng[:]))
                    mb = tmn[:, 0].rearrange("p (n o) -> p n o", o=1).broadcast_to([P, NT, SLICE])
                    rb = rng[:].rearrange("p (n o) -> p n o", o=1).broadcast_to([P, NT, SLICE])
                    link(V.tensor_tensor(u16[:], xsl[:], mb, ALU.subtract))
                    link(V.tensor_tensor(u16[:], u16[:], rb, ALU.mult))
                    link(V.tensor_scalar(u16[:], u16[:], 0.0, UMAX, ALU.max, ALU.min))
                    link(V.tensor_scalar(u16[:], u16[:], float(GRID), None, ALU.mult))
                    flat = u16[:].rearrange("p n j -> p (n j)")
                    ub = flat.rearrange("p (m o) -> p m o", o=1).broadcast_to([P, NT * SLICE, GRID])
                    gb = vec[:, V_GRID:V_GRID + GRID].rearrange("p (o g) -> p o g", o=1).broadcast_to([P, NT * SLICE, GRID])
                    hv = hot.rearrange("p n (j g) -> p (n j) g", g=GRID)
                    giv = gi[:].rearrange("p n j -> p (n j)")
                    link(V.tensor_tensor(hv, ub, gb, ALU.is_ge))
                    link(V.tensor_reduce(giv, hv[:, :, 1:GRID], X, ALU.add))
                    ib = giv.rearrange("p (m o) -> p m o", o=1).broadcast_to([P, NT * SLICE, GRID])
                    link(V.tensor_tensor(hv, ib, gb, ALU.is_equal))
                    link(V.tensor_tensor(flat, flat, giv, ALU.subtract))
                elif kind == "pick_turn":
                    V.tensor_copy(chT[:].rearrange("k n t -> k (n t)"), back[0:TILES, :]).then_inc(back_read, 1)
                elif kind == "pick":
                    f = task[1]
                    fs = slice(FG * f, FG * f + FG)
                    bv = big[:, :, 0:P]
                    for a in range(2):
                        last = V.tensor_tensor(bv[:, :, 64 * a:64 * a + 64],
                                               back[:].rearrange("p (n a m) -> p n a m", n=FG, a=2)[:, :, a],
                                               hot[:, fs], ALU.mult)
                    last.then_inc(back_read, 1)
                    dve.wait_ge(back_read, back_use(task) + 1)
                    for i in range(FG):
                        last = V.tensor_reduce(bsel[:, i].rearrange("p a j -> p (a j)"), bv[:, i].rearrange("p (m g) -> p m g", g=GRID), X, ALU.add)
                    link(last)
                    link(V.tensor_tensor(delta[:], bsel[:, :, 1], u16[:, fs], ALU.mult))
                    link(V.tensor_tensor(delta[:], delta[:], bsel[:, :, 0], ALU.add))
                    for i in range(FG):
                        ob = chosen[:, FG * f + i].rearrange("p (t o) -> p t o", o=1).broadcast_to([P, TILES, SLICE])
                        db = delta[:, i:i + 1].broadcast_to([P, TILES, SLICE])
                        last = V.tensor_tensor(big[:, i].rearrange("p (t j) -> p t j", j=SLICE), ob, db, ALU.mult)
                    link(last)
                    V.tensor_tensor(xs[:, fs], xs[:, fs], big[:], ALU.add).then_inc(delta_added, 1)
                    dve.wait_ge(delta_added, f + 1)

            dve.wait_ge(wn_in, 16)
            dve.wait_ge(tab_in, 16)
            for k in range(2):
                for w in range(2):
                    last = V.tensor_tensor(tab[:, :, k, w], tab_raw[:, :, k], wn[:, k, w:w + 1].broadcast_to([P, TB, D]), ALU.mult)
            link(last)
            dve.wait_ge(rows_in, 16)
            half = SLICE * GRID
            link(V.tensor_reduce(sgn[:], rows[:, half:2 * half].rearrange("k (j g) -> k j g", g=GRID), X, ALU.add))
            link(V.tensor_scalar(sgn[:], sgn[:], 1.0 / GRID, None, ALU.mult))
            link(V.tensor_scalar(sgn_ge[:], sgn[:], 0.0, -1.0, ALU.is_ge, ALU.add))
            link(V.scalar_tensor_tensor(sgn[:], sgn[:], 0.0, sgn_ge[:], ALU.is_gt, ALU.add))
            dve.wait_ge(ident_in, 16)
            V.tensor_tensor(sdiag[:], idn[0:TILES, 0:TILES].rearrange("k (t o) -> k t o", o=1).broadcast_to([TILES, TILES, SLICE]),
                            sgn[:].rearrange("k (o j) -> k o j", o=1).broadcast_to([TILES, TILES, SLICE]), ALU.mult).then_inc(signs_rhs, 1)
            link(V.tensor_scalar(rows[:, 0:2 * half], rows[:, 0:2 * half], rows[:, 2 * half:2 * half + 1], None, ALU.mult))
            dve.wait_ge(back_filled, 1)
            V.tensor_copy(ss[:].rearrange("p t j -> p (t j)"), back[:, 0:C]).then_inc(back_read, 1)

            for u in range(-1, NU + 2):
                if u >= 2 and UNITS[u - 2][1] == UNITS[u - 2][0] % TB:
                    s = UNITS[u - 2][0]
                    dve.wait_ge(pv_done, u - 1)
                    if s >= ORING:
                        dve.wait_ge(back_filled, back_use(("out_norm", s - ORING)) + 1)
                    V.tensor_copy(oT[:, s % ORING], oacc[:, s % 2]).then_inc(oacc_read, 1)
                for task in PLAN.get(u, ()):
                    do(task)


def kernel(**inputs):
    import concourse.bacc as bacc
    from concourse.bass_utils import run_bass_kernel_spmd

    a = {k: np.asarray(v) for k, v in inputs.items()}

    def tiled(w, n):
        return np.ascontiguousarray(w.reshape(n, P, -1).transpose(1, 0, 2))

    wproj = tiled(np.concatenate([a["L0_attn_Wq"], a["L0_attn_Wk"], a["L0_attn_Wv"]], 0).T, 2)
    tile_no = np.arange(TILES)
    tie = -(P * (tile_no // PER) + tile_no % PER).astype(np.float32)
    vectors = np.concatenate([a["L0_ffn_ln_gamma"], a["L0_ffn_ln_beta"], a["L0_attn_bo"], tie,
                              np.arange(GRID, dtype=np.float32)])
    inv_freq = (1.0 / 10000.0 ** (np.arange(0, D, 2, dtype=np.float32) / np.float32(D))).astype(np.float32)
    freqs = np.outer(np.arange(T, dtype=np.float32), inv_freq).astype(np.float32)
    cos, sin = np.cos(freqs), np.sin(freqs)
    tables = np.stack([np.concatenate([cos, cos], 1), np.concatenate([sin, -sin], 1)], 1)
    qw, kw = a["L0_attn_q_norm_w"], a["L0_attn_k_norm_w"]
    half = D // 2
    wnorm = np.stack([qw, kw, np.concatenate([qw[half:], qw[:half]]), np.concatenate([kw[half:], kw[:half]])])
    arrays = {
        "x": tiled(a["L0_attn_x"].reshape(NTOK, C), NT),
        "wproj": wproj,
        "wo": tiled(a["L0_attn_Wo"].T, 2),
        "vectors": np.ascontiguousarray(np.broadcast_to(vectors, (P, V_ALL))),
        "tables": np.ascontiguousarray(tables.reshape(TB, P, 2, D).transpose(1, 0, 2, 3)),
        "wnorm": np.ascontiguousarray(np.broadcast_to(wnorm.reshape(1, 2, 2, D), (P, 2, 2, D))),
        "grid_rows": np.ascontiguousarray(np.concatenate([
            a["L0_ffn_spline_bases"].reshape(TILES, -1), a["L0_ffn_spline_slopes"].reshape(TILES, -1),
            a["L0_ffn_output_scale"].reshape(TILES, 1)], 1)),
        "ident": np.eye(P, dtype=np.float32),
    }
    nc = bacc.Bacc("TRN2", target_bir_lowering=False, num_devices=1)
    args = [nc.dram_tensor(k, v.shape, mybir.dt.from_np(v.dtype), kind="ExternalInput").ap() for k, v in arrays.items()]
    out = nc.dram_tensor("out", (P, NT, C), mybir.dt.float32, kind="ExternalOutput").ap()
    build(nc, *args, out)
    r = run_bass_kernel_spmd(nc, [arrays], core_ids=[0])
    o = np.asarray(r.results[0]["out"])
    return np.ascontiguousarray(o.transpose(1, 0, 2)).reshape(B, T, C)
```

```python
from contextlib import ExitStack

import concourse.bass as bass
from concourse import mybir
import numpy as np

P = 128
B, T, C = 2, 1024, 256
NTOK = B * T
NT = NTOK // P
TB = T // P
H, G = 16, 4
D = C // H
R = H // G
HG = H + G
SLOTS = P // D
QKW = (H + G) * D
PROJ = QKW + G * D
VW = 32
SOFT_CAP = 50.0
MASKED = float(np.exp(np.float64(-SOFT_CAP)))
SCORE_SCALE = 1.0 / (np.sqrt(D) * SOFT_CAP)
RMS_EPS = 1e-6
LN_EPS = 1e-5
TILES, SLICE, GRID, CLUSTERS = 64, 4, 16, 8
PER = TILES // CLUSTERS
FG = 4
NF = NT // FG
BIG = 3.0e38
UMAX = float(np.float32(1.0 - 1e-6))
RSQRT_MAGIC = 1597463007.0
EARLY = 4
WARM = 30
PRING = 4
ORING = 4

UNITS = [(s, kb) for s in range(NT) for kb in range(s % TB + 1)]
NU = len(UNITS)
LAST = [max(u for u, (s, _) in enumerate(UNITS) if s == t) for t in range(NT)]

PLAN = {
    -1: [("norm_a", 0, 2), ("norm_a", 2, 2), ("norm_b", 0, 2), ("tables",), ("turn", 0, 2), ("project", 0),
        ("project", 1), ("norm_b", 2, 2), ("turn", 2, 2), ("project", 2), ("project", 3), ("rope_a", 0, 2),
        ("rope_b", 0, 2), ("rope_c", 0, 2), ("rope_a", 2, 2), ("cross",)],
    0: [("norm_a", 4, 4), ("rope_b", 2, 2), ("rope_c", 2, 2)],
    2: [("slopes",), ("norm_b", 4, 4), ("turn", 4, 2), ("signs",)],
    3: [("norm_a", 8, 4), ("project", 4), ("project", 5)],
    5: [("rope_a", 4, 2), ("rope_b", 4, 2), ("rope_c", 4, 2)],
    8: [("turn", 6, 2), ("project", 6)],
    9: [("project", 7), ("base_a", 0), ("base_b", 0)],
    10: [("rope_a", 6, 2)],
    11: [("suffix", 0), ("out_norm", 0)],
    12: [("rope_b", 6, 2)],
    13: [("out_turn", 0), ("out_project", 0)],
    14: [("norm_b", 8, 4), ("turn", 8, 2), ("out_norm", 1), ("rope_c", 6, 2)],
    15: [("out_turn", 1), ("project", 8)],
    16: [("project", 9), ("out_project", 1), ("turn", 10, 2), ("rope_a", 8, 2)],
    17: [("out_norm", 2), ("out_turn", 2)],
    18: [("out_norm", 3), ("out_project", 2), ("project", 10), ("out_turn", 3)],
    19: [("rope_b", 8, 2), ("rope_c", 8, 2)],
    20: [("base_a", 1), ("base_b", 1), ("out_norm", 4)],
    21: [("out_project", 3), ("project", 11), ("out_turn", 4), ("rope_a", 10, 2)],
    22: [("out_project", 4)],
    23: [("norm_a", 12, 4), ("out_norm", 5), ("out_turn", 5)],
    24: [("rope_b", 10, 2), ("rope_c", 10, 2), ("norm_b", 12, 4)],
    26: [("turn", 12, 2), ("out_project", 5)],
    27: [("project", 12)],
    28: [("project", 13), ("turn", 14, 2), ("rope_a", 12, 2)],
    29: [("out_norm", 6)],
    30: [("ffn_a", 0), ("out_turn", 6), ("project", 14)],
    31: [("base_a", 2), ("base_b", 2), ("project", 15)],
    32: [("rope_b", 12, 2), ("rope_c", 12, 2), ("out_project", 6)],
    33: [("rope_a", 14, 2)],
    35: [("rope_b", 14, 2)],
    36: [("rope_c", 14, 2)],
    37: [("base_a", 3)],
    38: [("base_b", 3), ("ffn_b", 0), ("ffn_shift", 0), ("out_norm", 7)],
    39: [("out_turn", 7), ("ffn_a", 1), ("suffix", 1)],
    40: [("ffn_c", 0), ("out_project", 7)],
    41: [("out_norm", 8), ("ffn_d", 0), ("ffn_b", 1), ("ffn_shift", 1), ("out_turn", 8), ("ffn_e", 0),
        ("ffn_least", 0), ("out_norm", 9)],
    42: [("ffn_a", 2), ("out_project", 8)],
    43: [("out_turn", 9), ("ffn_c", 1), ("out_project", 9)],
    44: [("ffn_b", 2), ("ffn_shift", 2), ("out_norm", 10)],
    45: [("ffn_d", 1), ("out_turn", 10)],
    46: [("ffn_a", 3), ("ffn_e", 1), ("ffn_least", 1), ("out_project", 10)],
    48: [("ffn_c", 2), ("out_norm", 11)],
    49: [("ffn_b", 3), ("ffn_shift", 3), ("ffn_d", 2), ("out_turn", 11), ("ffn_e", 2), ("ffn_least", 2)],
    50: [("out_project", 11)],
    53: [("ffn_c", 3), ("ffn_d", 3), ("ffn_e", 3), ("ffn_least", 3)],
    56: [("extremes",), ("extremes_row",), ("grid_a",)],
    57: [("grid_b",), ("grid_c",)],
    59: [("out_norm", 12)],
    60: [("pick_turn", 3)],
    61: [("pick", 3), ("pick_add", 3)],
    62: [("out_turn", 12)],
    63: [("out_norm", 13), ("pick_turn", 0)],
    64: [("out_project", 12), ("out_turn", 13), ("pick", 0), ("pick_add", 0)],
    65: [("out_project", 13), ("pick_turn", 1)],
    66: [("out_norm", 14), ("pick", 1), ("pick_add", 1)],
    67: [("out_turn", 14)],
    68: [("out_project", 14), ("pick_turn", 2)],
    72: [("pick", 2), ("pick_add", 2)],
    73: [("out_norm", 15), ("out_turn", 15), ("out_project", 15)],
}
TASKS = [t for ts in PLAN.values() for t in ts]
FRONT = ("turn", "project", "suffix")
BACK = ("signs", "out_norm", "out_turn", "out_project", "extremes", "extremes_row", "pick_turn", "pick")
FRONT_USES = [t for t in TASKS if t[0] in FRONT and not (t[0] == "project" and t[1] < EARLY)]
BACK_USES = [t for t in TASKS if t[0] in BACK]
STATS = [t for t in TASKS if t[0] in ("norm_a", "ffn_a")]
ROPES = [t for t in TASKS if t[0] == "rope_a"]
MVRING = 4
RAW = 4
PICKS = [t[1] for t in TASKS if t[0] == "pick"]
EARLY_F = tuple(f for f in range(NF) if TASKS.index(("pick", f)) < TASKS.index(("out_project", FG * f)))
assert all(f in EARLY_F or TASKS.index(("pick", f)) > TASKS.index(("out_project", FG * f + FG - 1)) for f in range(NF))

V_GAMMA, V_BETA, V_BO, V_KEY, V_GRID = 0, C, 2 * C, 3 * C, 3 * C + TILES
V_ALL = 3 * C + TILES + GRID


def build(nc, x, wproj, wo, vectors, tables, wnorm, grid_rows, ident, out):
    f32, bf16, i32 = mybir.dt.float32, mybir.dt.bfloat16, mybir.dt.int32
    ALU = mybir.AluOpType
    ACT = mybir.ActivationFunctionType
    X = mybir.AxisListType.X
    ctx = ExitStack()
    with ctx:
        def sb(name, shape, dt=f32):
            return ctx.enter_context(nc.sbuf_tensor(name, shape, dt))

        def pb(name, shape, dt=f32):
            return ctx.enter_context(nc.psum_tensor(name, shape, dt))

        def sem(name):
            return ctx.enter_context(nc.semaphore(name))

        xs = sb("xs", [P, NT, C])
        xn = sb("xn", [P, NT, C])
        xf = xn
        xnT = sb("xnT", [P, 2, 2, P])
        wproj_sb = sb("wproj_sb", [P, 2, PROJ])
        wo_sb = sb("wo_sb", [P, 2, C])
        vec = sb("vec", [P, V_ALL])
        tab = sb("tab", [P, TB, 2, 2, D])
        tab_raw = sb("tab_raw", [P, TB, 2, D])
        wn = sb("wn", [P, 2, 2, D])
        rows = sb("rows", [TILES, 2 * SLICE * GRID + 1])
        idn = sb("idn", [P, P])
        idb = sb("idb", [P, P], bf16)
        masked = sb("masked", [P, P])
        raw = sb("raw", [P, RAW, QKW])
        rot = sb("rot", [P, 2, 2, QKW])
        sq = sb("sq", [P, 2, QKW])
        tmp = sb("tmp", [P, 2, 2, QKW])
        parts = sb("parts", [P, 3, 2, QKW], bf16)
        combos = sb("combos", [P, 2, HG, SLOTS, D], bf16)
        qT = sb("qT", [P, TB, H, P], bf16)
        kT = sb("kT", [P, NT, G, P], bf16)
        val = sb("val", [P, NT, G, VW])
        suffix = sb("suffix", [P, B, TB - 1, G, D + 1])
        probs = sb("probs", [P, PRING, H, P])
        oT = sb("oT", [P, ORING, G * P])
        osum = sb("osum", [P, H, D + 1])
        oinv = sb("oinv", [P, H])
        y = sb("y", [P, C])
        yT = sb("yT", [P, 2, P])
        stats = sb("stats", [P, FG, 6])
        mv = sb("mv", [P, MVRING, FG, 2])
        rstd = sb("rstd", [P, MVRING, FG])
        ssq = sb("ssq", [P, 2, 2 * HG])
        rms = sb("rms", [P, 2, 2 * HG])
        newton = sb("newton", [P, 4, 2 * HG])
        newton_v = sb("newton_v", [P, 4, 2 * HG])
        big = sb("big", [P, FG, C])
        tsc = sb("tsc", [P, FG, TILES])
        key = sb("key", [P, FG, TILES])
        csc = sb("csc", [P, FG * CLUSTERS])
        best = sb("best", [P, FG])
        chosen = sb("chosen", [P, NT, TILES])
        xsl = sb("xsl", [P, NT, SLICE])
        ends = sb("ends", [P, 2, FG])
        cand = sb("cand", [P, 2, FG, TILES])
        low = sb("low", [P, 2, TILES])
        lowc = sb("lowc", [P, 1])
        lowb = sb("lowb", [P, P])
        lowr = sb("lowr", [P, 2, TILES])
        tmn = sb("tmn", [P, 2, NT])
        rng = sb("rng", [P, NT])
        u16 = sb("u16", [P, NT, SLICE])
        gi = sb("gi", [P, NT, SLICE])
        hot = xn[:, 0:NT * SLICE * GRID // C].rearrange("p a (b m) -> p (a b) m", m=SLICE * GRID)
        ss = sb("ss", [P, TILES, SLICE])
        sgn = sb("sgn", [TILES, SLICE])
        sgn_ge = sb("sgn_ge", [TILES, SLICE])
        sdiag = sb("sdiag", [TILES, TILES, SLICE])
        ones = sb("ones", [TILES, P])
        chT = sb("chT", [TILES, FG, P])
        bprod = sb("bprod", [P, FG, 2, SLICE * GRID])
        bsel = sb("bsel", [P, FG, 2, SLICE])
        delta = sb("delta", [P, FG, SLICE])

        scores = pb("scores", [P, H, P])
        oacc = pb("oacc", [P, 2, G * P])
        front = pb("front", [P, 512])
        back = pb("back", [P, 512])

        xchunks = [(0, 1), (1, 1), (2, 2), (4, 4), (8, 4), (12, 4)]
        x_in = [sem(f"x_in{i}") for i in range(len(xchunks))]
        ident_in, wproj_in, vec_in, tab_in, wn_in, wo_in, rows_in = (
            sem(n) for n in ("ident_in", "wproj_in", "vec_in", "tab_in", "wn_in", "wo_in", "rows_in"))
        tab_ready = sem("tab_ready")
        const_ready = sem("const_ready")
        xn_ready = sem("xn_ready")
        front_filled, front_read = sem("front_filled"), sem("front_read")
        back_filled, back_read = sem("back_filled"), sem("back_read")
        combos_ready = sem("combos_ready")
        turned = sem("turned")
        idb_ready = sem("idb_ready")
        early_filled = sem("early_filled")
        early_read = sem("early_read")
        crossed = sem("crossed")
        cross_read_act, cross_read_dve = sem("cross_read_act"), sem("cross_read_dve")
        scores_ready, tanh_done, exp_done, mask_done, pv_done = (
            sem(n) for n in ("scores_ready", "tanh_done", "exp_done", "mask_done", "pv_done"))
        oacc_read = sem("oacc_read")
        dve_chain = sem("dve_chain")
        pool_chain = sem("pool_chain")
        stats_ready = sem("stats_ready")
        rstd_ready = sem("rstd_ready")
        sq_ready = sem("sq_ready")
        sin_ready = sem("sin_ready")
        cos_ready = sem("cos_ready")
        ssq_ready = sem("ssq_ready")
        rms_ready = sem("rms_ready")
        normed2 = sem("normed2")
        xf_ready = sem("xf_ready")
        base_ready = sem("base_ready")
        signs_ready = sem("signs_ready")
        signed = sem("signed")
        choice_ready = sem("choice_ready")
        slice_ready = sem("slice_ready")
        lowb_ready = sem("lowb_ready")
        signs_rhs = sem("signs_rhs")
        y_ready = sem("y_ready")
        delta_ready = sem("delta_ready")
        delta_added = sem("delta_added")
        out_done = sem("out_done")

        cross_bf = scores[:].rearrange("p h q -> p (h q)").bitcast(bf16)

        front_use, back_use = FRONT_USES.index, BACK_USES.index

        def projected(engine, t):
            if t < EARLY:
                engine.wait_ge(early_read, t + 1)
            else:
                engine.wait_ge(front_read, front_use(("project", t)) + 1)

        block = ctx.enter_context(nc.Block())

        @block.sync
        def _(sp):
            sp.dma_start(xs[:, 0:1], x[:, 0:1]).then_inc(x_in[0], 16)
            sp.dma_start(wproj_sb[:], wproj).then_inc(wproj_in, 16)
            sp.dma_start(xs[:, 1:2], x[:, 1:2]).then_inc(x_in[1], 16)
            for i in range(2, len(xchunks)):
                t0, n = xchunks[i]
                sp.dma_start(xs[:, t0:t0 + n], x[:, t0:t0 + n]).then_inc(x_in[i], 16)
            for t in range(1, NT):
                sp.wait_ge(combos_ready, t + 1)
                if t > 1:
                    sp.wait_ge(turned, 32 * (t - 1))
                if t >= TB:
                    sp.wait_ge(scores_ready, LAST[t - TB] + 1)
                sp.dma_start_transpose(qT[:, t % TB], combos[:, t % 2, 0:H].rearrange("p h s d -> p (h s d)"))\
                    .then_inc(turned, 16)
                sp.wait_ge(turned, 32 * t - 16)
                sp.dma_start_transpose(kT[:, t], combos[:, t % 2, H:HG].rearrange("p h s d -> p (h s d)"))\
                    .then_inc(turned, 16)
            n_out = 0
            for f in range(NF):
                if f not in EARLY_F:
                    sp.wait_ge(delta_added, PICKS.index(f) + 1)
                    sp.dma_start(out[:, FG * f:FG * f + FG], xs[:, FG * f:FG * f + FG]).then_inc(out_done, 16)
                    n_out += 1
            for f in EARLY_F:
                for t in range(FG * f, FG * f + FG):
                    sp.wait_ge(back_read, back_use(("out_project", t)) + 1)
                    sp.dma_start(out[:, t], xs[:, t]).then_inc(out_done, 16)
                    n_out += 1
            sp.wait_ge(out_done, 16 * n_out)

        @block.gpsimd
        def _(pool):
            nc.gpsimd.memset(masked[:], MASKED).then_inc(const_ready, 1)
            nc.gpsimd.memset(ones[:], 1.0).then_inc(const_ready, 1)
            nc.gpsimd.memset(val[:, :, :, D:VW], 0.0).then_inc(pool_chain, 1)
            pool.wait_ge(pool_chain, 1)
            nc.gpsimd.memset(val[:, :, :, D:D + 1], 1.0).then_inc(const_ready, 1)
            chain = [1]

            def link(ins):
                chain[0] += 1
                ins.then_inc(pool_chain, 1)
                pool.wait_ge(pool_chain, chain[0])

            def every(v0):
                return vec[:, v0:v0 + C].rearrange("p (o c) -> p o c", o=1).broadcast_to([P, FG, C])

            POOL = nc.gpsimd

            def rsqrt(v, n):
                g0, a, b = (newton[:, k, 0:n] for k in range(3))
                link(POOL.tensor_scalar(g0.bitcast(i32), v.bitcast(i32), -0.5, RSQRT_MAGIC, ALU.mult, ALU.add))
                for _ in range(3):
                    link(POOL.tensor_tensor(a, v, g0, ALU.mult))
                    link(POOL.tensor_tensor(b, a, g0, ALU.mult))
                    link(POOL.tensor_scalar(b, b, -0.5, 1.5, ALU.mult, ALU.add))
                    link(POOL.tensor_tensor(g0, b, g0, ALU.mult))
                return g0

            def variance(task):
                k, n = STATS.index(task), FG if task[0] == "ffn_a" else task[2]
                if k == 0:
                    return
                pool.wait_ge(stats_ready, k + 1)
                v = newton[:, 3, 0:n]
                link(POOL.tensor_scalar(v, mv[:, k % MVRING, 0:n, 1], LN_EPS, None, ALU.add))
                r = rsqrt(v, n)
                POOL.tensor_copy(rstd[:, k % MVRING, 0:n], r).then_inc(rstd_ready, 1)

            def head_rms(t0, n):
                k, m = ROPES.index(("rope_a", t0, n)), n * HG
                qk = raw[:, t0 % RAW:t0 % RAW + n]
                projected(pool, t0 + n - 1)
                if t0 >= EARLY:
                    pool.wait_ge(ssq_ready, k)
                    POOL.tensor_tensor(sq[:, 0:n], qk, qk, ALU.mult).then_inc(sq_ready, 1)
                if k >= 2:
                    t1, n1 = ROPES[k - 2][1:]
                    pool.wait_ge(combos_ready, t1 + n1)
                if k == 0:
                    pool.wait_ge(tab_ready, 1)
                heads = qk.rearrange("p n (h d) -> p n h d", d=D)
                rv = rot[:, k % 2, 0:n].rearrange("p n (h d) -> p n h d", d=D)
                for w, (h0, h1) in enumerate(((0, H), (H, HG))):
                    cos = tab[:, t0 % TB:t0 % TB + n, 0, w:w + 1, :].broadcast_to([P, n, h1 - h0, D])
                    last = POOL.tensor_tensor(rv[:, :, h0:h1], heads[:, :, h0:h1], cos, ALU.mult)
                last.then_inc(cos_ready, 1)
                if k == 0:
                    return
                pool.wait_ge(ssq_ready, k + 1)
                mean, r = newton[:, 3, 0:m], rms[:, k % 2, 0:m]
                link(POOL.tensor_scalar(mean, ssq[:, k % 2, 0:m], 1.0 / D, None, ALU.mult))
                g0 = rsqrt(mean, m)
                link(POOL.tensor_tensor(r, mean, g0, ALU.mult))
                POOL.tensor_scalar(r, r, RMS_EPS, None, ALU.add).then_inc(rms_ready, 1)

            for u in range(-1, NU + 2):
                if 1 <= u <= NU and UNITS[u - 1][1] == UNITS[u - 1][0] % TB:
                    pool.wait_ge(exp_done, u)
                    pr = probs[:, (u - 1) % PRING]
                    POOL.affine_select(out=pr, in_=pr, pattern=[[0, H], [1, P]], compare_op=ALU.is_ge,
                                       fill=MASKED, base=0, channel_multiplier=-1).then_inc(mask_done, 1)
                for task in PLAN.get(u, ()):
                    kind = task[0]
                    f = task[1] if len(task) == 2 else None
                    fs = slice(FG * f, FG * f + FG) if kind in (
                        "base_a", "base_b", "ffn_b", "ffn_shift", "ffn_c", "ffn_d", "pick", "pick_add") else None
                    if kind in ("norm_a", "ffn_a"):
                        variance(task)
                    elif kind == "rope_a":
                        head_rms(*task[1:])
                    elif kind == "base_a":
                        pool.wait_ge(xn_ready, FG * f + FG)
                        link(POOL.tensor_tensor(xs[:, fs], xs[:, fs], xn[:, fs], ALU.add))
                    elif kind == "base_b":
                        if f == 0:
                            pool.wait_ge(vec_in, 16)
                        POOL.tensor_tensor(xs[:, fs], xs[:, fs], every(V_BO), ALU.add).then_inc(base_ready, 1)
                    elif kind == "ffn_b":
                        pool.wait_ge(normed2, f + 1)
                        link(POOL.tensor_tensor(xf[:, fs], xf[:, fs], every(V_GAMMA), ALU.mult))
                    elif kind == "ffn_shift":
                        POOL.tensor_tensor(xf[:, fs], xf[:, fs], every(V_BETA), ALU.add).then_inc(xf_ready, 1)
                    elif kind == "ffn_c":
                        pool.wait_ge(signs_ready, f + 1)
                        slopes = ss[:].rearrange("p (o t) j -> p o (t j)", o=1).broadcast_to([P, FG, C])
                        POOL.tensor_tensor(big[:], big[:], slopes, ALU.mult).then_inc(signed, 1)
                    elif kind == "ffn_d":
                        pool.wait_ge(choice_ready, f + 1)
                        POOL.tensor_tensor(big[:].rearrange("p n (t j) -> p (n t) j", j=SLICE),
                                           xf[:, fs].rearrange("p n (t j) -> p (n t) j", j=SLICE),
                                           chosen[:, fs].rearrange("p n (t o) -> p (n t) o", o=1)
                                           .broadcast_to([P, FG * TILES, SLICE]), ALU.mult).then_inc(slice_ready, 1)
                    elif kind == "pick":
                        pool.wait_ge(delta_ready, PICKS.index(f) + 1)
                        if PICKS.index(f):
                            pool.wait_ge(delta_added, PICKS.index(f))
                        for i in range(FG):
                            ob = chosen[:, FG * f + i].rearrange("p (t o) -> p t o", o=1).broadcast_to([P, TILES, SLICE])
                            db = delta[:, i:i + 1].broadcast_to([P, TILES, SLICE])
                            last = POOL.tensor_tensor(big[:, i].rearrange("p (t j) -> p t j", j=SLICE), ob, db, ALU.mult)
                        link(last)
                    elif kind == "pick_add":
                        if f not in EARLY_F:
                            pool.wait_ge(back_read, back_use(("out_project", FG * f + FG - 1)) + 1)
                        POOL.tensor_tensor(xs[:, fs], xs[:, fs], big[:], ALU.add).then_inc(delta_added, 1)

        @block.scalar
        def _(act):
            act.dma_start(idn[:], ident).then_inc(ident_in, 16)
            act.dma_start(wn[:], wnorm).then_inc(wn_in, 16)
            act.dma_start(tab_raw[:], tables).then_inc(tab_in, 16)
            act.dma_start(vec[:], vectors).then_inc(vec_in, 16)
            act.dma_start(rows[:], grid_rows).then_inc(rows_in, 16)
            act.dma_start(wo_sb[:], wo).then_inc(wo_in, 16)
            nc.scalar.preload_act_table(ACT.Tanh)
            act.wait_ge(const_ready, 3)
            for t in range(EARLY):
                act.wait_ge(early_filled, t + 1)
                bank = scores[:, R * t:R * t + R].rearrange("p r q -> p (r q)")
                nc.scalar.copy(raw[:, t], bank[:, 0:QKW])
                if t % 2 == 0 and t:
                    act.wait_ge(ssq_ready, t // 2)
                ins = nc.scalar.activation(sq[:, t % 2], bank[:, 0:QKW], ACT.Square)
                if t % 2:
                    ins.then_inc(sq_ready, 1)
                nc.scalar.copy(val[:, t, :, 0:D], bank[:, QKW:PROJ].rearrange("p (g d) -> p g d", g=G)).then_inc(early_read, 1)
            act.wait_ge(crossed, 1)
            nc.scalar.copy(qT[:, 0, 0:H // 2], cross_bf[:, 0:P * H // 2].rearrange("p (h q) -> p h q", q=P)).then_inc(cross_read_act, 1)
            for u in range(NU):
                pr = probs[:, u % PRING]
                act.wait_ge(scores_ready, u + 1)
                if u >= PRING:
                    act.wait_ge(pv_done, u - PRING + 1)
                nc.scalar.activation(pr, scores[:], ACT.Tanh, scale=SCORE_SCALE).then_inc(tanh_done, 1)
                act.wait_ge(tanh_done, u + 1)
                nc.scalar.activation(pr, pr, ACT.Exp, scale=SOFT_CAP).then_inc(exp_done, 1)

        @block.tensor
        def _(pe):
            def take_front(task):
                n = front_use(task)
                if n:
                    pe.wait_ge(front_read, n)

            def take_back(task):
                n = back_use(task)
                if n:
                    pe.wait_ge(back_read, n)

            def score(u):
                s, kb = UNITS[u]
                kt = s - s % TB + kb
                if u == 0:
                    pe.wait_ge(cross_read_act, 1)
                    pe.wait_ge(cross_read_dve, 1)
                elif kb == 0:
                    pe.wait_ge(turned, 32 * s)
                if u:
                    pe.wait_ge(tanh_done, u)
                for g in range(G):
                    last = nc.tensor.matmul(scores[:, R * g:R * g + R, :], kT[:, kt, g, :],
                                            qT[:, s % TB, R * g:R * g + R, :], start=True, stop=True)
                last.then_inc(scores_ready, 1)

            def value(u):
                s, kb = UNITS[u]
                kt = s - s % TB + kb
                pe.wait_ge(exp_done, u + 1)
                if kb == s % TB:
                    pe.wait_ge(mask_done, s + 1)
                if kb == 0 and s >= 2:
                    pe.wait_ge(oacc_read, s - 1)
                if u == 0:
                    pe.wait_ge(const_ready, 3)
                projected(pe, kt)
                for g in range(G):
                    for r in range(R):
                        last = nc.tensor.matmul(oacc[VW * r:VW * r + VW, s % 2, P * g:P * g + P],
                                                val[:, kt, g, :], probs[:, u % PRING, R * g + r, :],
                                                start=(kb == 0 and g == 0), stop=(kb == s % TB),
                                                skip_group_check=True)
                last.then_inc(pv_done, 1)

            def do(task):
                kind = task[0]
                if kind == "turn":
                    t, n = task[1:]
                    take_front(task)
                    pe.wait_ge(xn_ready, t + n)
                    if t == 0:
                        pe.wait_ge(ident_in, 16)
                    for i in range(n):
                        for c in range(2):
                            o = P * (2 * i + c)
                            last = nc.tensor.transpose(front[:, o:o + P], xn[:, t + i, P * c:P * c + P], idn[:])
                    last.then_inc(front_filled, 1)
                elif kind == "signs":
                    pe.wait_ge(signs_rhs, 1)
                    pe.wait_ge(const_ready, 2)
                    nc.tensor.matmul(back[:, 0:C], ones[:], sdiag[:].rearrange("k t j -> k (t j)"),
                                     start=True, stop=True).then_inc(back_filled, 1)
                elif kind == "project":
                    t = task[1]
                    if t < EARLY:
                        pe.wait_ge(front_read, t // 2 + 1)
                        bank, filled = scores[:, R * t:R * t + R].rearrange("p r q -> p (r q)"), early_filled
                    else:
                        take_front(task)
                        bank, filled = front, front_filled
                    if t == 0:
                        pe.wait_ge(wproj_in, 16)
                    for c in range(2):
                        last = nc.tensor.matmul(bank[:, 0:PROJ], xnT[:, t % 2, c], wproj_sb[:, c], start=(c == 0), stop=(c == 1))
                    last.then_inc(filled, 1)
                elif kind == "cross":
                    pe.wait_ge(combos_ready, 1)
                    pe.wait_ge(early_read, EARLY)
                    pe.wait_ge(idb_ready, 1)
                    for h in range(HG):
                        last = nc.tensor.transpose(cross_bf[:, P * h:P * h + P], combos[:, 0, h].rearrange("p s d -> p (s d)"), idb[:])
                    last.then_inc(crossed, 1)
                elif kind == "suffix":
                    b = task[1]
                    take_front(task)
                    for qt in range(TB - 1):
                        for kb in range(qt + 1, TB):
                            o = qt * G * (D + 1)
                            last = nc.tensor.matmul(front[:, o:o + G * (D + 1)].rearrange("p (g d) -> p g d", g=G),
                                                    masked[:], val[:, TB * b + kb, :, 0:D + 1],
                                                    start=(kb == qt + 1), stop=(kb == TB - 1))
                    last.then_inc(front_filled, 1)
                elif kind == "out_norm":
                    s = task[1]
                    take_back(task)
                    pe.wait_ge(oacc_read, s + 1)
                    for g in range(G):
                        last = nc.tensor.transpose(back[:, P * g:P * g + P], oT[:, s % ORING, P * g:P * g + P], idn[:])
                    last.then_inc(back_filled, 1)
                elif kind == "out_turn":
                    take_back(task)
                    pe.wait_ge(y_ready, task[1] + 1)
                    for c in range(2):
                        last = nc.tensor.transpose(back[:, P * c:P * c + P], y[:, P * c:P * c + P], idn[:])
                    last.then_inc(back_filled, 1)
                elif kind == "out_project":
                    if task[1] == 0:
                        pe.wait_ge(wo_in, 16)
                    take_back(task)
                    for c in range(2):
                        last = nc.tensor.matmul(back[:, 0:C], yT[:, c], wo_sb[:, c], start=(c == 0), stop=(c == 1))
                    last.then_inc(back_filled, 1)
                elif kind == "extremes":
                    take_back(task)
                    pe.wait_ge(lowb_ready, 1)
                    nc.tensor.transpose(back[:, 0:P], low[:].rearrange("p a t -> p (a t)"), idn[:]).then_inc(back_filled, 1)
                elif kind == "extremes_row":
                    take_back(task)
                    nc.tensor.matmul(back[:, 0:P], lowb[:], idn[:], start=True, stop=True).then_inc(back_filled, 1)
                elif kind == "pick_turn":
                    f = task[1]
                    take_back(task)
                    for i in range(FG):
                        last = nc.tensor.transpose(back[0:TILES, P * i:P * i + P], chosen[:, FG * f + i, :], idn[:])
                    last.then_inc(back_filled, 1)
                elif kind == "pick":
                    take_back(task)
                    for i in range(FG):
                        last = nc.tensor.matmul(back[:, P * i:P * i + P], chT[:, i], rows[:, 0:P], start=True, stop=True)
                    last.then_inc(back_filled, 1)

            pe.wait_ge(const_ready, 1)
            for _ in range(WARM):
                nc.tensor.matmul(back[:, 0:P], masked[:], masked[:], start=True, stop=True)
            for u in range(-1, NU + 2):
                if 0 <= u < NU:
                    score(u)
                if u >= 2:
                    value(u - 2)
                for task in PLAN.get(u, ()):
                    do(task)

        @block.vector
        def _(dve):
            chain = [0]

            def link(ins):
                chain[0] += 1
                ins.then_inc(dve_chain, 1)
                dve.wait_ge(dve_chain, chain[0])

            V = nc.vector

            def rsqrt(v, n):
                g0, a, b = (newton_v[:, j, 0:n] for j in range(3))
                link(V.tensor_scalar(g0.bitcast(i32), v.bitcast(i32), -0.5, RSQRT_MAGIC, ALU.mult, ALU.add))
                for _ in range(3):
                    link(V.tensor_tensor(a, v, g0, ALU.mult))
                    link(V.scalar_tensor_tensor(b, a, -0.5, g0, ALU.mult, ALU.mult))
                    link(V.scalar_tensor_tensor(g0, b, 1.5, g0, ALU.add, ALU.mult))
                return g0

            def moments(src, t0, n, k):
                if k > MVRING:
                    dve.wait_ge(rstd_ready, k - MVRING)
                if k:
                    dve.wait_ge(stats_ready, k)
                for i in range(n):
                    last = V.bn_stats(stats[:, i], src[:, t0 + i])
                link(last)
                for i in range(n):
                    last = V.bn_aggr(mv[:, k % MVRING, i], stats[:, i])
                last.then_inc(stats_ready, 1)

            def center(src, dst, t0, n, k):
                if k:
                    dve.wait_ge(rstd_ready, k)
                for i in range(n):
                    yield V.tensor_scalar(dst[:, t0 + i], src[:, t0 + i], mv[:, k % MVRING, i, 0:1],
                                          rstd[:, k % MVRING, i:i + 1], ALU.subtract, ALU.mult)

            def rope_a(t0, n):
                k, m, half = ROPES.index(("rope_a", t0, n)), n * HG, D // 2
                heads = raw[:, t0 % RAW:t0 % RAW + n].rearrange("p n (h d) -> p n h d", d=D)
                tv = tmp[:, k % 2, 0:n].rearrange("p n (h d) -> p n h d", d=D)
                projected(dve, t0 + n - 1)
                for w, (h0, h1) in enumerate(((0, H), (H, HG))):
                    for lo, hi in ((0, half), (half, D)):
                        sin = tab[:, t0 % TB:t0 % TB + n, 1, w:w + 1, lo:hi].broadcast_to([P, n, h1 - h0, half])
                        last = V.tensor_tensor(tv[:, :, h0:h1, lo:hi], heads[:, :, h0:h1, D - hi:D - lo], sin, ALU.mult)
                last.then_inc(sin_ready, 1)
                dve.wait_ge(sq_ready, k + 1)
                V.tensor_reduce(ssq[:, k % 2, 0:m], sq[:, 0:n].rearrange("p n (h d) -> p (n h) d", d=D), X, ALU.add)\
                    .then_inc(ssq_ready, 1)
                if k == 0:
                    dve.wait_ge(ssq_ready, 1)
                    mean, r = newton_v[:, 3, 0:m], rms[:, 0, 0:m]
                    link(V.tensor_scalar(mean, ssq[:, 0, 0:m], 1.0 / D, None, ALU.mult))
                    g0 = rsqrt(mean, m)
                    link(V.tensor_tensor(r, mean, g0, ALU.mult))
                    link(V.tensor_scalar(r, r, RMS_EPS, None, ALU.add))

            def lay(t0, n, j, q_slots, k_slots, done=None):
                for i in range(n):
                    c = combos[:, (t0 + i) % 2]
                    for h0, h1, places in ((0, H, q_slots), (H, HG, k_slots)):
                        count = len(range(SLOTS)[places])
                        v = parts[:, j, i, D * h0:D * h1].rearrange("p (h o d) -> p h o d", o=1, d=D)
                        last = V.tensor_copy(c[:, h0:h1, places], v.broadcast_to([P, h1 - h0, count, D]))
                    if done is not None:
                        last.then_inc(done, 1)

            def rope_b(t0, n):
                k, m = ROPES.index(("rope_a", t0, n)), n * HG
                dve.wait_ge(sin_ready, k + 1)
                dve.wait_ge(cos_ready, k + 1)
                V.tensor_tensor(rot[:, k % 2, 0:n], rot[:, k % 2, 0:n], tmp[:, k % 2, 0:n], ALU.add).then_inc(dve_chain, 1)
                chain[0] += 1
                if k:
                    dve.wait_ge(rms_ready, k)
                inv, rr = ssq[:, k % 2, 0:m], rot[:, k % 2, 0:n]
                link(V.reciprocal(inv, rms[:, k % 2, 0:m]))
                rall = rr.rearrange("p n (h d) -> p (n h) d", d=D)
                link(V.tensor_tensor(rall, rall, inv.rearrange("p (h o) -> p h o", o=1).broadcast_to([P, m, D]), ALU.mult))
                p1 = parts[:, 0, 0:n]
                link(V.tensor_copy(p1, rr))
                V.tensor_tensor(rr, rr, p1, ALU.subtract).then_inc(dve_chain, 1)
                chain[0] += 1
                if t0 + n > 3:
                    dve.wait_ge(turned, 32 * (t0 + n - 3))
                lay(t0, n, 0, slice(0, 3), slice(0, 7, 3))

            def rope_c(t0, n):
                k = ROPES.index(("rope_a", t0, n))
                rr, p2, p3 = rot[:, k % 2, 0:n], parts[:, 1, 0:n], parts[:, 2, 0:n]
                dve.wait_ge(dve_chain, chain[0])
                link(V.tensor_copy(p2, rr))
                V.tensor_tensor(p3, rr, p2, ALU.subtract).then_inc(dve_chain, 1)
                chain[0] += 1
                lay(t0, n, 1, slice(3, 6), slice(1, 8, 3))
                dve.wait_ge(dve_chain, chain[0])
                lay(t0, n, 2, slice(6, 8), slice(2, 6, 3), combos_ready)

            def ffn_choose(f):
                fs = slice(FG * f, FG * f + FG)
                dve.wait_ge(signed, f + 1)
                link(V.tensor_reduce(tsc[:].rearrange("p n t -> p (n t)"), big[:].rearrange("p n (t j) -> p (n t) j", j=SLICE), X, ALU.add))
                link(V.tensor_reduce(csc[:], tsc[:].rearrange("p n (c k) -> p (n c) k", k=PER), X, ALU.add))
                kc = vec[:, V_KEY:V_KEY + TILES].rearrange("p (o t) -> p o t", o=1).broadcast_to([P, FG, TILES])
                link(V.scalar_tensor_tensor(key[:], tsc[:], float(PER), kc, ALU.mult, ALU.add))
                k3 = key[:].rearrange("p n (c k) -> p (n c) k", k=PER)
                cb = csc[:].rearrange("p (c o) -> p c o", o=1).broadcast_to([P, FG * CLUSTERS, PER])
                link(V.scalar_tensor_tensor(k3, cb, float(PER * P), k3, ALU.mult, ALU.add))
                link(V.tensor_reduce(best[:], key[:], X, ALU.max))
                bb = best[:].rearrange("p (n o) -> p n o", o=1).broadcast_to([P, FG, TILES])
                V.tensor_tensor(chosen[:, fs], key[:], bb, ALU.is_equal).then_inc(choice_ready, 1)

            def ffn_extremes(f):
                fs = slice(FG * f, FG * f + FG)
                oh = chosen[:, fs]
                dve.wait_ge(slice_ready, f + 1)
                link(V.tensor_reduce(xsl[:, fs], big[:].rearrange("p n (t j) -> p n j t", j=SLICE), X, ALU.add))
                V.tensor_reduce(ends[:, 0], xsl[:, fs], X, ALU.min)
                link(V.tensor_reduce(ends[:, 1], xsl[:, fs], X, ALU.max))
                link(V.tensor_scalar(ends[:, 1], ends[:, 1], -1.0, None, ALU.mult))
                for a in range(2):
                    eb = ends[:, a].rearrange("p (n o) -> p n o", o=1).broadcast_to([P, FG, TILES])
                    V.tensor_tensor(cand[:, a], oh, eb, ALU.mult)
                link(V.tensor_scalar(key[:], oh, -BIG, BIG, ALU.mult, ALU.add))
                for a in range(2):
                    last = V.tensor_tensor(cand[:, a], cand[:, a], key[:], ALU.add)
                link(last)

            def ffn_least(f):
                least = low if f == 0 else key
                for a in range(2):
                    last = V.tensor_reduce(least[:, a], cand[:, a].rearrange("p n t -> p t n"), X, ALU.min)
                link(last)
                if f:
                    ins = V.tensor_tensor(low[:], low[:], key[:, 0:2], ALU.min)
                    if f == NF - 1:
                        ins.then_inc(lowb_ready, 1)
                    else:
                        link(ins)

            def do(task):
                kind = task[0]
                if task in FRONT_USES:
                    dve.wait_ge(front_filled, front_use(task) + 1)
                if kind in BACK:
                    dve.wait_ge(back_filled, back_use(task) + 1)
                if kind == "norm_a":
                    t0, n = task[1:]
                    for i, (c0, cn) in enumerate(xchunks):
                        if c0 < t0 + n and t0 < c0 + cn:
                            dve.wait_ge(x_in[i], 16)
                    k = STATS.index(task)
                    moments(xs, t0, n, k)
                    if k == 0:
                        dve.wait_ge(stats_ready, 1)
                        link(V.tensor_scalar(newton_v[:, 3, 0:n], mv[:, 0, 0:n, 1], LN_EPS, None, ALU.add))
                        link(V.tensor_copy(rstd[:, 0, 0:n], rsqrt(newton_v[:, 3, 0:n], n)))
                elif kind == "norm_b":
                    t0, n = task[1:]
                    for ins in center(xs, xn, t0, n, STATS.index(("norm_a", t0, n))):
                        ins.then_inc(xn_ready, 1)
                elif kind == "turn":
                    n = task[2]
                    V.tensor_copy(xnT[:, task[1] % 2:task[1] % 2 + n].rearrange("p i c t -> p (i c t)"), front[:, 0:C * n]).then_inc(front_read, 1)
                elif kind == "project":
                    t = task[1]
                    if t < EARLY:
                        return
                    if t == EARLY:
                        dve.wait_ge(const_ready, 3)
                    if t >= RAW:
                        dve.wait_ge(cos_ready, next(k for k, (_, t0, n) in enumerate(ROPES) if t0 + n > t - RAW) + 1)
                    V.tensor_copy(val[:, t, :, 0:D], front[:, QKW:PROJ].rearrange("p (g d) -> p g d", g=G))
                    V.tensor_copy(raw[:, t % RAW], front[:, 0:QKW]).then_inc(front_read, 1)
                    dve.wait_ge(front_read, front_use(task) + 1)
                elif kind == "tables":
                    dve.wait_ge(ident_in, 16)
                    V.tensor_copy(idb[:], idn[:]).then_inc(idb_ready, 1)
                    dve.wait_ge(wn_in, 16)
                    dve.wait_ge(tab_in, 16)
                    for k in range(2):
                        for w in range(2):
                            last = V.tensor_tensor(tab[:, :, k, w], tab_raw[:, :, k], wn[:, k, w:w + 1].broadcast_to([P, TB, D]), ALU.mult)
                    last.then_inc(tab_ready, 1)
                elif kind == "slopes":
                    dve.wait_ge(rows_in, 16)
                    half = SLICE * GRID
                    link(V.tensor_reduce(sgn[:], rows[:, half:2 * half].rearrange("k (j g) -> k j g", g=GRID), X, ALU.add))
                    link(V.tensor_scalar(sgn[:], sgn[:], 1.0 / GRID, None, ALU.mult))
                    link(V.tensor_scalar(sgn_ge[:], sgn[:], 0.0, -1.0, ALU.is_ge, ALU.add))
                    link(V.scalar_tensor_tensor(sgn[:], sgn[:], 0.0, sgn_ge[:], ALU.is_gt, ALU.add))
                    dve.wait_ge(ident_in, 16)
                    V.tensor_tensor(sdiag[:], idn[0:TILES, 0:TILES].rearrange("k (t o) -> k t o", o=1).broadcast_to([TILES, TILES, SLICE]),
                                    sgn[:].rearrange("k (o j) -> k o j", o=1).broadcast_to([TILES, TILES, SLICE]), ALU.mult).then_inc(signs_rhs, 1)
                    link(V.tensor_scalar(rows[:, 0:2 * half], rows[:, 0:2 * half], rows[:, 2 * half:2 * half + 1], None, ALU.mult))
                elif kind == "cross":
                    dve.wait_ge(crossed, 1)
                    half = P * H // 2
                    V.tensor_copy(qT[:, 0, H // 2:H], cross_bf[:, half:2 * half].rearrange("p (h q) -> p h q", q=P))
                    V.tensor_copy(kT[:, 0], cross_bf[:, 2 * half:P * HG].rearrange("p (h q) -> p h q", q=P)).then_inc(cross_read_dve, 1)
                elif kind == "rope_a":
                    rope_a(*task[1:])
                elif kind == "rope_b":
                    rope_b(*task[1:])
                elif kind == "rope_c":
                    rope_c(*task[1:])
                elif kind == "signs":
                    V.tensor_copy(ss[:].rearrange("p t j -> p (t j)"), back[:, 0:C]).then_inc(back_read, 1)
                elif kind == "suffix":
                    V.tensor_copy(suffix[:, task[1]].rearrange("p q g d -> p (q g d)"),
                                  front[:, 0:(TB - 1) * G * (D + 1)]).then_inc(front_read, 1)
                elif kind == "out_norm":
                    s = task[1]
                    b, qt = divmod(s, TB)
                    acc = back[:].rearrange("p (g r w) -> p g r w", g=G, w=VW)
                    dst = osum[:].rearrange("p (g r) d -> p g r d", g=G)
                    if s:
                        dve.wait_ge(y_ready, s)
                    if qt < TB - 1:
                        if qt == 0:
                            dve.wait_ge(front_read, front_use(("suffix", b)) + 1)
                        sfx = suffix[:, b, qt].rearrange("p g (o d) -> p g o d", o=1).broadcast_to([P, G, R, D + 1])
                        ins = V.tensor_tensor(dst, acc[:, :, :, 0:D + 1], sfx, ALU.add)
                    else:
                        ins = V.tensor_copy(dst, acc[:, :, :, 0:D + 1])
                    ins.then_inc(back_read, 1)
                    dve.wait_ge(back_read, back_use(task) + 1)
                    link(V.reciprocal(oinv[:], osum[:, :, D]))
                    ob = oinv[:].rearrange("p (h o) -> p h o", o=1).broadcast_to([P, H, D])
                    V.tensor_tensor(y[:].rearrange("p (h d) -> p h d", d=D), osum[:, :, 0:D], ob, ALU.mult).then_inc(y_ready, 1)
                elif kind == "out_turn":
                    V.tensor_copy(yT[:].rearrange("p c t -> p (c t)"), back[:, 0:C]).then_inc(back_read, 1)
                elif kind == "out_project":
                    s = task[1]
                    dve.wait_ge(base_ready, s // FG + 1)
                    if s // FG in EARLY_F:
                        dve.wait_ge(delta_added, PICKS.index(s // FG) + 1)
                    V.tensor_tensor(xs[:, s], xs[:, s], back[:, 0:C], ALU.add).then_inc(back_read, 1)
                elif kind == "ffn_a":
                    f = task[1]
                    moments(xn, FG * f, FG, STATS.index(task))
                elif kind == "ffn_b":
                    f = task[1]
                    dve.wait_ge(base_ready, f + 1)
                    tile = next(t for t in FRONT_USES if t[0] == "turn" and t[1] + t[2] == FG * f + FG)
                    dve.wait_ge(front_filled, front_use(tile) + 1)
                    for i, ins in enumerate(center(xn, xf, FG * f, FG, STATS.index(("ffn_a", f)))):
                        if i == FG - 1:
                            ins.then_inc(normed2, 1)
                elif kind == "ffn_c":
                    f = task[1]
                    fs = slice(FG * f, FG * f + FG)
                    dve.wait_ge(xf_ready, f + 1)
                    link(V.tensor_scalar(big[:], xf[:, fs], 0.0, -1.0, ALU.is_ge, ALU.add))
                    V.scalar_tensor_tensor(big[:], xf[:, fs], 0.0, big[:], ALU.is_gt, ALU.add).then_inc(signs_ready, 1)
                elif kind == "ffn_d":
                    ffn_choose(task[1])
                elif kind == "ffn_e":
                    ffn_extremes(task[1])
                elif kind == "ffn_least":
                    ffn_least(task[1])
                elif kind == "extremes":
                    link(V.tensor_reduce(lowc[:], back[:, 0:P], X, ALU.min))
                    V.tensor_scalar(lowb[:], masked[:], 0.0, lowc[:], ALU.mult, ALU.add).then_inc(back_read, 1)
                elif kind == "extremes_row":
                    V.tensor_copy(lowr[:].rearrange("p a t -> p (a t)"), back[:, 0:P]).then_inc(back_read, 1)
                    dve.wait_ge(back_read, back_use(task) + 1)
                elif kind == "grid_a":
                    wide = big[:].rearrange("p a c -> p (a c)").rearrange("p (n t) -> p n t", n=NT)
                    for a in range(2):
                        lb = lowr[:, a:a + 1].broadcast_to([P, NT, TILES])
                        link(V.tensor_tensor(wide, chosen[:], lb, ALU.mult))
                        link(V.tensor_reduce(tmn[:, a], wide, X, ALU.add))
                    link(V.scalar_tensor_tensor(rng[:], tmn[:, 1], -1.0, tmn[:, 0], ALU.mult, ALU.subtract))
                    link(V.tensor_scalar(rng[:], rng[:], 1e-8, None, ALU.add))
                    link(V.reciprocal(rng[:], rng[:]))
                elif kind == "grid_b":
                    mb = tmn[:, 0].rearrange("p (n o) -> p n o", o=1).broadcast_to([P, NT, SLICE])
                    rb = rng[:].rearrange("p (n o) -> p n o", o=1).broadcast_to([P, NT, SLICE])
                    link(V.tensor_tensor(u16[:], xsl[:], mb, ALU.subtract))
                    link(V.tensor_tensor(u16[:], u16[:], rb, ALU.mult))
                    link(V.tensor_scalar(u16[:], u16[:], 0.0, UMAX, ALU.max, ALU.min))
                    link(V.tensor_scalar(u16[:], u16[:], float(GRID), None, ALU.mult))
                elif kind == "grid_c":
                    flat = u16[:].rearrange("p n j -> p (n j)")
                    ub = flat.rearrange("p (m o) -> p m o", o=1).broadcast_to([P, NT * SLICE, GRID])
                    gb = vec[:, V_GRID:V_GRID + GRID].rearrange("p (o g) -> p o g", o=1).broadcast_to([P, NT * SLICE, GRID])
                    hv = hot.rearrange("p n (j g) -> p (n j) g", g=GRID)
                    giv = gi[:].rearrange("p n j -> p (n j)")
                    link(V.tensor_tensor(hv, ub, gb, ALU.is_ge))
                    link(V.tensor_reduce(giv, hv[:, :, 1:GRID], X, ALU.add))
                    ib = giv.rearrange("p (m o) -> p m o", o=1).broadcast_to([P, NT * SLICE, GRID])
                    link(V.tensor_tensor(hv, ib, gb, ALU.is_equal))
                    link(V.tensor_tensor(flat, flat, giv, ALU.subtract))
                elif kind == "pick_turn":
                    V.tensor_copy(chT[:].rearrange("k n t -> k (n t)"), back[0:TILES, :]).then_inc(back_read, 1)
                elif kind == "pick":
                    f = task[1]
                    fs = slice(FG * f, FG * f + FG)
                    picked = hot[:, fs]
                    if PICKS.index(f):
                        dve.wait_ge(delta_added, PICKS.index(f))
                    for a in range(2):
                        last = V.tensor_tensor(bprod[:, :, a], back[:].rearrange("p (n a m) -> p n a m", n=FG, a=2)[:, :, a],
                                               picked, ALU.mult)
                    last.then_inc(back_read, 1)
                    dve.wait_ge(back_read, back_use(task) + 1)
                    link(V.tensor_reduce(bsel[:].rearrange("p n a j -> p (n a j)"),
                                         bprod[:].rearrange("p n a (j g) -> p (n a j) g", g=GRID), X, ALU.add))
                    link(V.tensor_tensor(delta[:], bsel[:, :, 1], u16[:, fs], ALU.mult))
                    V.tensor_tensor(delta[:], delta[:], bsel[:, :, 0], ALU.add).then_inc(delta_ready, 1)

            for u in range(-1, NU + 2):
                if u >= 2 and UNITS[u - 2][1] == UNITS[u - 2][0] % TB:
                    s = UNITS[u - 2][0]
                    dve.wait_ge(pv_done, u - 1)
                    if s >= ORING:
                        dve.wait_ge(back_filled, back_use(("out_norm", s - ORING)) + 1)
                    V.tensor_copy(oT[:, s % ORING], oacc[:, s % 2]).then_inc(oacc_read, 1)
                for task in PLAN.get(u, ()):
                    do(task)


def kernel(**inputs):
    import concourse.bacc as bacc
    from concourse.bass_utils import run_bass_kernel_spmd

    a = {k: np.asarray(v) for k, v in inputs.items()}

    def tiled(w, n):
        return np.ascontiguousarray(w.reshape(n, P, -1).transpose(1, 0, 2))

    wproj = tiled(np.concatenate([a["L0_attn_Wq"], a["L0_attn_Wk"], a["L0_attn_Wv"]], 0).T, 2)
    tile_no = np.arange(TILES)
    tie = -(P * (tile_no // PER) + tile_no % PER).astype(np.float32)
    vectors = np.concatenate([a["L0_ffn_ln_gamma"], a["L0_ffn_ln_beta"], a["L0_attn_bo"], tie,
                              np.arange(GRID, dtype=np.float32)])
    inv_freq = (1.0 / 10000.0 ** (np.arange(0, D, 2, dtype=np.float32) / np.float32(D))).astype(np.float32)
    freqs = np.outer(np.arange(T, dtype=np.float32), inv_freq).astype(np.float32)
    cos, sin = np.cos(freqs), np.sin(freqs)
    tables = np.stack([np.concatenate([cos, cos], 1), np.concatenate([sin, -sin], 1)], 1)
    qw, kw = a["L0_attn_q_norm_w"], a["L0_attn_k_norm_w"]
    half = D // 2
    wnorm = np.stack([qw, kw, np.concatenate([qw[half:], qw[:half]]), np.concatenate([kw[half:], kw[:half]])])
    arrays = {
        "x": tiled(a["L0_attn_x"].reshape(NTOK, C), NT),
        "wproj": wproj,
        "wo": tiled(a["L0_attn_Wo"].T, 2),
        "vectors": np.ascontiguousarray(np.broadcast_to(vectors, (P, V_ALL))),
        "tables": np.ascontiguousarray(tables.reshape(TB, P, 2, D).transpose(1, 0, 2, 3)),
        "wnorm": np.ascontiguousarray(np.broadcast_to(wnorm.reshape(1, 2, 2, D), (P, 2, 2, D))),
        "grid_rows": np.ascontiguousarray(np.concatenate([
            a["L0_ffn_spline_bases"].reshape(TILES, -1), a["L0_ffn_spline_slopes"].reshape(TILES, -1),
            a["L0_ffn_output_scale"].reshape(TILES, 1)], 1)),
        "ident": np.eye(P, dtype=np.float32),
    }
    nc = bacc.Bacc("TRN2", target_bir_lowering=False, num_devices=1)
    args = [nc.dram_tensor(k, v.shape, mybir.dt.from_np(v.dtype), kind="ExternalInput").ap() for k, v in arrays.items()]
    out = nc.dram_tensor("out", (P, NT, C), mybir.dt.float32, kind="ExternalOutput").ap()
    build(nc, *args, out)
    r = run_bass_kernel_spmd(nc, [arrays], core_ids=[0])
    o = np.asarray(r.results[0]["out"])
    return np.ascontiguousarray(o.transpose(1, 0, 2)).reshape(B, T, C)
```

```python
from contextlib import ExitStack

import concourse.bass as bass
from concourse import mybir
import numpy as np

P = 128
B, T, C = 2, 1024, 256
NTOK = B * T
NT = NTOK // P
TB = T // P
H, G = 16, 4
D = C // H
R = H // G
HG = H + G
SLOTS = P // D
SUFFIX = (range(0, TB // 2), range(TB // 2, TB))
LAYS = (((0, H, slice(0, 3)), (H, HG, slice(0, 7, 3))),
        ((0, H, slice(3, 6)), (H, HG, slice(1, 8, 3))),
        ((0, H, slice(6, 8)), (H, HG, slice(2, 6, 3))))
QKW = (H + G) * D
PROJ = QKW + G * D
VW = 32
SOFT_CAP = 50.0
MASKED = float(np.exp(np.float64(-SOFT_CAP)))
SCORE_SCALE = 1.0 / (np.sqrt(D) * SOFT_CAP)
RMS_EPS = 1e-6
LN_EPS = 1e-5
TILES, SLICE, GRID, CLUSTERS = 64, 4, 16, 8
PER = TILES // CLUSTERS
FG = 4
NF = NT // FG
BIG = 3.0e38
UMAX = float(np.float32(1.0 - 1e-6))
RSQRT_MAGIC = 1597463007.0
EARLY = 4
CROSSED = 2
WARM = 30
REWARM = 32
PRING = 4
HALF = P // 2
PACK = R * HALF + R // 2 * HALF
QRING = 7
LAG = 3
ORING = 4

UNITS = [(s, kb) for s in range(NT) for kb in [s % TB] + list(range(s % TB))]
NU = len(UNITS)
LAST = [max(u for u, (s, _) in enumerate(UNITS) if s == t) for t in range(NT)]
FIRST = [min(u for u, (s, _) in enumerate(UNITS) if s == t) for t in range(NT)]

PLAN = {
    -1: [("norm_a", 0, 2), ("norm_b", 0, 2), ("norm_a", 2, 2), ("turn", 0, 2), ("project", 0), ("slopes",),
        ("tables",), ("norm_b", 2, 2), ("project", 1), ("turn", 2, 2), ("rope_a", 0, 2), ("norm_a", 4, 4),
        ("rope_b", 0, 1), ("project", 2), ("project", 3), ("rope_a", 2, 2), ("rope_split", 0, 1), ("rope_c", 0, 1),
        ("rope_b", 1, 1), ("rope_d", 0, 1), ("rope_split", 1, 1), ("rope_c", 1, 1), ("cross", 0), ("rope_d", 1, 1),
        ("norm_b", 4, 4), ("rope_b", 2, 1), ("cross", 1), ("rope_split", 2, 1), ("rope_c", 2, 1), ("rope_d", 2, 1),
        ("rope_b", 3, 1), ("rope_split", 3, 1), ("mask", 0), ("rope_c", 3, 1)],
    0: [("turn", 4, 2), ("norm_a", 8, 4)],
    2: [("drain", 0), ("rope_d", 3, 1), ("project_a", 4), ("project", 4)],
    3: [("project_a", 5), ("project", 5), ("signs",)],
    5: [("mask", 1), ("rope_a", 4, 2), ("mask", 2), ("turn", 6, 2), ("drain", 1), ("project_a", 6), ("rope_b", 4, 2),
        ("project", 6), ("project_a", 7), ("project", 7)],
    6: [("rope_split", 4, 2), ("rope_c", 4, 2), ("rope_d", 4, 2)],
    7: [("sums", 0)],
    8: [("suffix", 0, 0), ("out_norm", 0)],
    9: [("base_a", 0), ("drain", 2), ("out_turn", 0), ("mask", 3), ("rope_a", 6, 2), ("rope_b", 6, 2),
        ("rope_split", 6, 2), ("rope_c", 6, 2)],
    10: [("suffix", 0, 1)],
    11: [("rope_d", 6, 2), ("mask", 4)],
    12: [("base_b", 0), ("drain", 3), ("norm_b", 8, 4), ("mask", 5)],
    14: [("out_project", 0)],
    15: [("turn", 8, 2), ("out_norm", 1)],
    16: [("project_a", 8), ("project", 8), ("out_turn", 1)],
    17: [("out_norm", 2), ("drain", 4), ("out_project", 1), ("project_a", 9), ("project", 9), ("turn", 10, 2),
        ("rope_a", 8, 2)],
    18: [("out_turn", 2), ("out_norm", 3)],
    19: [("out_project", 2)],
    20: [("rope_b", 8, 2), ("out_turn", 3), ("rope_split", 8, 2)],
    21: [("out_project", 3), ("base_a", 1), ("base_a", 2), ("base_b", 1), ("project_a", 10)],
    22: [("rope_c", 8, 2), ("rope_d", 8, 2), ("project", 10)],
    23: [("mask", 6), ("drain", 5), ("out_norm", 4), ("project_a", 11), ("project", 11), ("rope_a", 10, 2)],
    24: [("out_turn", 4), ("norm_a", 12, 4), ("out_norm", 5), ("rope_b", 10, 2)],
    25: [("out_project", 4), ("rope_split", 10, 2), ("norm_b", 12, 4), ("rope_c", 10, 2)],
    26: [("base_b", 2)],
    28: [("turn", 12, 2), ("project_a", 12), ("project", 12), ("project_a", 13), ("rope_d", 10, 2), ("project", 13),
        ("base_a", 3), ("base_b", 3)],
    29: [("rope_a", 12, 2), ("turn", 14, 2), ("drain", 6), ("mask", 7)],
    30: [("out_turn", 5), ("project_a", 14), ("project", 14), ("ffn_a", 0), ("out_project", 5), ("project_a", 15),
        ("project", 15), ("out_norm", 6)],
    31: [("rope_b", 12, 2), ("out_turn", 6)],
    32: [("rope_split", 12, 2), ("rope_c", 12, 2)],
    33: [("rope_d", 12, 2), ("rope_a", 14, 2), ("rope_b", 14, 2), ("rope_split", 14, 2)],
    34: [("rope_c", 14, 2)],
    35: [("sums", 1), ("out_project", 6)],
    36: [("suffix", 1, 0), ("mask", 8)],
    37: [("rope_d", 14, 2)],
    38: [("mask", 9), ("ffn_b", 0), ("drain", 7), ("ffn_shift", 0), ("ffn_a", 1), ("drain", 8)],
    39: [("suffix", 1, 1), ("out_norm", 7), ("out_turn", 7), ("out_project", 7)],
    40: [("ffn_c", 0), ("out_norm", 8)],
    41: [("mask", 10)],
    42: [("ffn_d", 0), ("ffn_b", 1), ("ffn_pick", 0), ("drain", 9)],
    43: [("ffn_a", 2)],
    44: [("ffn_shift", 1), ("ffn_e", 0), ("ffn_cand", 0), ("out_turn", 8), ("out_norm", 9), ("out_project", 8),
        ("mask", 11), ("ffn_least", 0), ("out_turn", 9), ("ffn_c", 1), ("out_project", 9), ("ffn_b", 2),
        ("ffn_a", 3)],
    46: [("ffn_d", 1), ("ffn_pick", 1)],
    47: [("drain", 10), ("ffn_shift", 2), ("out_norm", 10), ("out_turn", 10)],
    48: [("ffn_e", 1), ("drain", 11), ("out_project", 10)],
    49: [("ffn_cand", 1), ("mask", 12), ("ffn_least", 1), ("out_norm", 11)],
    50: [("ffn_c", 2)],
    52: [("ffn_b", 3), ("ffn_d", 2), ("ffn_pick", 2), ("out_turn", 11), ("ffn_e", 2), ("mask", 13), ("drain", 12)],
    53: [("ffn_cand", 2), ("ffn_shift", 3), ("out_project", 11), ("ffn_least", 2)],
    54: [("ffn_c", 3), ("ffn_d", 3), ("ffn_pick", 3), ("ffn_e", 3), ("ffn_cand", 3)],
    55: [("ffn_least", 3)],
    58: [("out_norm", 12)],
    59: [("mask", 14), ("extremes",), ("extremes_row",), ("grid_a",), ("grid_b",)],
    60: [("drain", 13)],
    61: [("pick_turn", 3)],
    62: [("grid_c",), ("pick", 3)],
    63: [("out_turn", 12), ("pick_add", 3), ("out_norm", 13)],
    64: [("pick_turn", 0), ("pick", 0)],
    65: [("out_project", 12), ("out_turn", 13), ("mask", 15)],
    66: [("drain", 14), ("pick_add", 0), ("out_project", 13)],
    67: [("pick_turn", 1)],
    68: [("out_norm", 14)],
    69: [("pick", 1), ("pick_add", 1)],
    70: [("pick_turn", 2), ("out_turn", 14)],
    71: [("pick", 2)],
    72: [("out_project", 14)],
    74: [("pick_add", 2), ("drain", 15), ("out_norm", 15), ("out_turn", 15), ("out_project", 15)],
}
TASKS = [t for ts in PLAN.values() for t in ts]
IN_PSUM = ("turn", "project", "suffix", "signs", "out_norm", "out_turn", "out_project", "extremes", "extremes_row",
           "pick_turn", "pick")
USES = [t for t in TASKS if t[0] in IN_PSUM and not (t[0] == "project" and t[1] < EARLY)]
STATS = [t for t in TASKS if t[0] in ("norm_a", "ffn_a")]
ROPES = [t for t in TASKS if t[0] == "rope_a"]
SPLITS = [t for t in TASKS if t[0] == "rope_split"]
MVRING = 4
RAW = 4
PICKS = [t[1] for t in TASKS if t[0] == "pick"]
EARLY_F = tuple(f for f in range(NF) if TASKS.index(("pick", f)) < TASKS.index(("out_project", FG * f)))
assert all(f in EARLY_F or TASKS.index(("pick", f)) > TASKS.index(("out_project", FG * f + FG - 1)) for f in range(NF))

V_GAMMA, V_BETA, V_BO, V_KEY, V_GRID = 0, C, 2 * C, 3 * C, 3 * C + TILES
V_ALL = 3 * C + TILES + GRID


def build(nc, x, wproj, wo, vectors, tables, wnorm, grid_rows, ident, out):
    f32, bf16, i32 = mybir.dt.float32, mybir.dt.bfloat16, mybir.dt.int32
    ALU = mybir.AluOpType
    ACT = mybir.ActivationFunctionType
    X = mybir.AxisListType.X
    ctx = ExitStack()
    with ctx:
        def sb(name, shape, dt=f32):
            return ctx.enter_context(nc.sbuf_tensor(name, shape, dt))

        def pb(name, shape, dt=f32):
            return ctx.enter_context(nc.psum_tensor(name, shape, dt))

        def sem(name):
            return ctx.enter_context(nc.semaphore(name))

        xs = sb("xs", [P, NT, C])
        xn = sb("xn", [P, NT, C])
        xf = xn
        xnT = sb("xnT", [P, 2, 2, P])
        wproj_sb = sb("wproj_sb", [P, 2, PROJ])
        wo_sb = sb("wo_sb", [P, 2, C])
        vec = sb("vec", [P, V_ALL])
        tab = sb("tab", [P, TB, 2, 2, D])
        tab_raw = sb("tab_raw", [P, TB, 2, D])
        wn = sb("wn", [P, 2, 2, D])
        rows = sb("rows", [TILES, 2 * SLICE * GRID + 1])
        idn = sb("idn", [P, P])
        idb = sb("idb", [P, P], bf16)
        masked = sb("masked", [P, P])
        raw = sb("raw", [P, RAW, QKW])
        rot = sb("rot", [P, 2, 2, QKW])
        sq = sb("sq", [P, 2, QKW])
        tmp = sb("tmp", [P, 2, 2, QKW])
        parts = sb("parts", [P, 3, 2, QKW], bf16)
        combos = sb("combos", [P, 2, HG, SLOTS, D], bf16)
        qT = sb("qT", [P, QRING, H, P], bf16)
        kT = sb("kT", [P, NT, G, P], bf16)
        val = sb("val", [P, NT, G, VW])
        val_low = sb("val_low", [P, NT, G, VW])
        masked_high = sb("masked_high", [P, P])
        suffix = sb("suffix", [P, B, TB, G, D + 1])
        probs = sb("probs", [P, PRING, H, P])
        oT = sb("oT", [P, ORING, G * P])
        osum = sb("osum", [P, H, D + 1])
        oinv = sb("oinv", [P, H])
        y = sb("y", [P, C])
        yT = sb("yT", [P, 2, P])
        stats = sb("stats", [P, FG, 6])
        mv = sb("mv", [P, MVRING, FG, 2])
        rstd = sb("rstd", [P, MVRING, FG])
        ssq = sb("ssq", [P, 2, 2 * HG])
        rms = sb("rms", [P, 2, 2 * HG])
        newton = sb("newton", [P, 4, 2 * HG])
        newton_v = sb("newton_v", [P, 4, 2 * HG])
        big = sb("big", [P, FG, C])
        tsc = sb("tsc", [P, FG, TILES])
        key = sb("key", [P, FG, TILES])
        csc = sb("csc", [P, FG * CLUSTERS])
        best = sb("best", [P, FG])
        chosen = sb("chosen", [P, NT, TILES])
        xsl = sb("xsl", [P, NT, SLICE])
        ends = sb("ends", [P, 2, FG])
        cand = sb("cand", [P, 2, FG, TILES])
        low = sb("low", [P, 2, TILES])
        lowc = sb("lowc", [P, 1])
        lowb = sb("lowb", [P, P])
        lowr = sb("lowr", [P, 2, TILES])
        tmn = sb("tmn", [P, 2, NT])
        rng = sb("rng", [P, NT])
        u16 = sb("u16", [P, NT, SLICE])
        gi = sb("gi", [P, NT, SLICE])
        hot = xn[:, 0:NT * SLICE * GRID // C].rearrange("p a (b m) -> p (a b) m", m=SLICE * GRID)
        ss = sb("ss", [P, TILES, SLICE])
        sgn = sb("sgn", [TILES, SLICE])
        sgn_ge = sb("sgn_ge", [TILES, SLICE])
        ones = sb("ones", [TILES, P])
        chT = sb("chT", [TILES, FG, P])
        sdiag = chT[:, 0:2].rearrange("k a (t j) -> k (a t) j", j=SLICE)
        bprod = cand[:].rearrange("p a n t -> p (a n t)").rearrange("p (n a m) -> p n a m", n=FG, a=2)
        bsel = sb("bsel", [P, FG, 2, SLICE])
        delta = sb("delta", [P, FG, SLICE])

        scores = pb("scores", [P, H, P])
        oacc = pb("oacc", [P, 2, G * P])
        banks = pb("bank0", [P, 512]), pb("bank1", [P, 512])

        xchunks = [(0, 1), (1, 1), (2, 2), (4, 4), (8, 4), (12, 4)]
        x_in = [sem(f"x_in{i}") for i in range(len(xchunks))]
        ident_in, wproj_in, vec_in, tab_in, wn_in, wo_in, rows_in = (
            sem(n) for n in ("ident_in", "wproj_in", "vec_in", "tab_in", "wn_in", "wo_in", "rows_in"))
        tab_ready = sem("tab_ready")
        const_ready = sem("const_ready")
        xn_ready = sem("xn_ready")
        filled, read = sem("filled"), sem("read")
        combos_ready = sem("combos_ready")
        turned = sem("turned")
        idb_ready = sem("idb_ready")
        first_parts = sem("first_parts")
        lay_done = sem("lay_done")
        early_filled = sem("early_filled")
        early_read = sem("early_read")
        crossed = sem("crossed")
        cross_read_act, cross_read_dve = sem("cross_read_act"), sem("cross_read_dve")
        scores_ready, tanh_done, exp_done, mask_done, pv_done = (
            sem(n) for n in ("scores_ready", "tanh_done", "exp_done", "mask_done", "pv_done"))
        oacc_read = sem("oacc_read")
        dve_chain = sem("dve_chain")
        pool_chain = sem("pool_chain")
        stats_ready = sem("stats_ready")
        rstd_ready = sem("rstd_ready")
        sq_ready = sem("sq_ready")
        sin_ready = sem("sin_ready")
        cos_ready = sem("cos_ready")
        ssq_ready = sem("ssq_ready")
        rms_ready = sem("rms_ready")
        normed2 = sem("normed2")
        xf_ready = sem("xf_ready")
        base_ready = sem("base_ready")
        signs_ready = sem("signs_ready")
        signed = sem("signed")
        choice_ready = sem("choice_ready")
        slice_ready = sem("slice_ready")
        lowb_ready = sem("lowb_ready")
        signs_rhs = sem("signs_rhs")
        sums_ready = sem("sums_ready")
        y_ready = sem("y_ready")
        delta_ready = sem("delta_ready")
        delta_added = sem("delta_added")
        out_done = sem("out_done")

        cross_bf = scores[:].rearrange("p h q -> p (h q)").bitcast(bf16)
        cross_q = cross_bf[:, 0:P * H], oacc[:].rearrange("p a q -> p (a q)").bitcast(bf16)
        cross_k = cross_bf[:, P * H:P * HG], banks[1][:, 0:P * G // 2].bitcast(bf16)

        use = USES.index

        def projected(engine, t):
            if t < EARLY:
                engine.wait_ge(early_read, t + 1)
            else:
                engine.wait_ge(read, use(("project", t)) + 1)

        def packed(t):
            bank = t.rearrange("p (g r) q -> p g (r q)", g=G)
            return (bank[:, :, 0:R * HALF].rearrange("p g (r q) -> p g r q", q=HALF),
                    bank[:, :, R * HALF:PACK].rearrange("p g (r q) -> p g r q", q=HALF))

        def used(t, u):
            if UNITS[u][1] < UNITS[u][0] % TB:
                return t
            return t.rearrange("p (g r) q -> p g (r q)", g=G)[:, :, 0:PACK]

        block = ctx.enter_context(nc.Block())

        @block.sync
        def _(sp):
            sp.dma_start(xs[:, 0:1], x[:, 0:1]).then_inc(x_in[0], 16)
            sp.dma_start(wproj_sb[:], wproj).then_inc(wproj_in, 16)
            sp.dma_start(xs[:, 1:2], x[:, 1:2]).then_inc(x_in[1], 16)
            for i in range(2, len(xchunks)):
                t0, n = xchunks[i]
                sp.dma_start(xs[:, t0:t0 + n], x[:, t0:t0 + n]).then_inc(x_in[i], 16)
            for t in range(CROSSED, NT):
                sp.wait_ge(combos_ready, t + 1)
                if t > CROSSED:
                    sp.wait_ge(turned, 32 * (t - CROSSED))
                if t >= QRING:
                    sp.wait_ge(scores_ready, LAST[t - QRING] + 1)
                sp.dma_start_transpose(qT[:, t % QRING], combos[:, t % 2, 0:H].rearrange("p h s d -> p (h s d)"))\
                    .then_inc(turned, 16)
                sp.wait_ge(turned, 32 * (t - CROSSED) + 16)
                sp.dma_start_transpose(kT[:, t], combos[:, t % 2, H:HG].rearrange("p h s d -> p (h s d)"))\
                    .then_inc(turned, 16)
            n_out = 0
            for f in range(NF):
                if f not in EARLY_F:
                    sp.wait_ge(delta_added, PICKS.index(f) + 1)
                    sp.dma_start(out[:, FG * f:FG * f + FG], xs[:, FG * f:FG * f + FG]).then_inc(out_done, 16)
                    n_out += 1
            for f in EARLY_F:
                for t in range(FG * f, FG * f + FG):
                    sp.wait_ge(read, use(("out_project", t)) + 1)
                    sp.dma_start(out[:, t], xs[:, t]).then_inc(out_done, 16)
                    n_out += 1
            sp.wait_ge(out_done, 16 * n_out)

        @block.gpsimd
        def _(pool):
            nc.gpsimd.memset(masked[:], MASKED).then_inc(const_ready, 1)
            nc.gpsimd.memset(ones[:], 1.0).then_inc(const_ready, 1)
            nc.gpsimd.memset(masked_high[:], 0.0)
            nc.gpsimd.memset(val_low[:, :, :, D:VW], 0.0)
            nc.gpsimd.memset(val[:, :, :, D:VW], 0.0).then_inc(pool_chain, 1)
            pool.wait_ge(pool_chain, 1)
            nc.gpsimd.memset(val_low[:, :, :, D:D + 1], 1.0)
            nc.gpsimd.memset(val[:, :, :, D:D + 1], 1.0).then_inc(const_ready, 1)
            pool.wait_ge(const_ready, 3)
            nc.gpsimd.memset(masked_high[HALF:P, 0:HALF], MASKED).then_inc(const_ready, 1)
            pool.wait_ge(const_ready, 4)
            chain = [1]

            def link(ins):
                chain[0] += 1
                ins.then_inc(pool_chain, 1)
                pool.wait_ge(pool_chain, chain[0])

            def every(v0):
                return vec[:, v0:v0 + C].rearrange("p (o c) -> p o c", o=1).broadcast_to([P, FG, C])

            POOL = nc.gpsimd

            def rsqrt(v, n):
                g0, a, b = (newton[:, k, 0:n] for k in range(3))
                link(POOL.tensor_scalar(g0.bitcast(i32), v.bitcast(i32), -0.5, RSQRT_MAGIC, ALU.mult, ALU.add))
                for _ in range(3):
                    link(POOL.tensor_tensor(a, v, g0, ALU.mult))
                    link(POOL.tensor_tensor(b, a, g0, ALU.mult))
                    link(POOL.tensor_scalar(b, b, -0.5, 1.5, ALU.mult, ALU.add))
                    link(POOL.tensor_tensor(g0, b, g0, ALU.mult))
                return g0

            def variance(task):
                k, n = STATS.index(task), FG if task[0] == "ffn_a" else task[2]
                if k == 0:
                    return
                pool.wait_ge(stats_ready, k + 1)
                v = newton[:, 3, 0:n]
                link(POOL.tensor_scalar(v, mv[:, k % MVRING, 0:n, 1], LN_EPS, None, ALU.add))
                r = rsqrt(v, n)
                POOL.tensor_copy(rstd[:, k % MVRING, 0:n], r).then_inc(rstd_ready, 1)

            def head_rms(t0, n):
                k, m = ROPES.index(("rope_a", t0, n)), n * HG
                qk = raw[:, t0 % RAW:t0 % RAW + n]
                projected(pool, t0 + n - 1)
                if t0 >= EARLY:
                    pool.wait_ge(ssq_ready, k)
                    POOL.tensor_tensor(sq[:, 0:n], qk, qk, ALU.mult).then_inc(sq_ready, 1)
                if k >= 2:
                    t1, n1 = ROPES[k - 2][1:]
                    pool.wait_ge(combos_ready, t1 + n1)
                if k == 0:
                    pool.wait_ge(tab_ready, 1)
                heads = qk.rearrange("p n (h d) -> p n h d", d=D)
                rv = rot[:, k % 2, 0:n].rearrange("p n (h d) -> p n h d", d=D)
                for w, (h0, h1) in enumerate(((0, H), (H, HG))):
                    cos = tab[:, t0 % TB:t0 % TB + n, 0, w:w + 1, :].broadcast_to([P, n, h1 - h0, D])
                    last = POOL.tensor_tensor(rv[:, :, h0:h1], heads[:, :, h0:h1], cos, ALU.mult)
                last.then_inc(cos_ready, 1)
                if k == 0:
                    return
                pool.wait_ge(ssq_ready, k + 1)
                mean, r = newton[:, 3, 0:m], rms[:, k % 2, 0:m]
                link(POOL.tensor_scalar(mean, ssq[:, k % 2, 0:m], 1.0 / D, None, ALU.mult))
                g0 = rsqrt(mean, m)
                link(POOL.tensor_tensor(r, mean, g0, ALU.mult))
                POOL.tensor_scalar(r, r, RMS_EPS, None, ALU.add).then_inc(rms_ready, 1)

            def mask(s):
                m = FIRST[s]
                pool.wait_ge(exp_done, m + 1)
                hi, lo = packed(probs[:, m % PRING])
                POOL.affine_select(out=hi, in_=hi, pattern=[[0, G], [0, R], [1, HALF]], compare_op=ALU.is_ge,
                                   fill=MASKED, base=HALF, channel_multiplier=-1)
                pattern = [[0, G], [0, R // 2], [1, HALF]]
                link(POOL.affine_select(out=lo[0:HALF], in_=lo[0:HALF], pattern=pattern, compare_op=ALU.is_ge,
                                        fill=MASKED, base=0, channel_multiplier=-1))
                POOL.affine_select(out=lo[HALF:P], in_=lo[HALF:P], pattern=pattern, compare_op=ALU.is_ge,
                                   fill=MASKED, base=0, channel_multiplier=-1).then_inc(mask_done, 1)
                pool.wait_ge(mask_done, s + 1)

            for u in range(-1, NU + LAG):
                for task in PLAN.get(u, ()):
                    kind = task[0]
                    f = task[1] if len(task) == 2 else None
                    fs = slice(FG * f, FG * f + FG) if kind in (
                        "base_a", "base_b", "ffn_b", "ffn_shift", "ffn_pick", "pick", "pick_add") else None
                    if kind == "mask":
                        mask(task[1])
                    elif kind == "sums":
                        b = task[1]
                        projected(pool, TB * b + TB - 1)

                        def tile(t):
                            return val[:, TB * b + t, :, 0:D + 1]

                        link(POOL.tensor_copy(suffix[:, b, TB - 2], tile(TB - 1)))
                        for qt in range(TB - 3, -1, -1):
                            ins = POOL.tensor_tensor(suffix[:, b, qt], suffix[:, b, qt + 1], tile(qt + 1), ALU.add)
                            if qt:
                                link(ins)
                        ins.then_inc(sums_ready, 1)
                    elif kind in ("norm_a", "ffn_a"):
                        variance(task)
                    elif kind == "rope_a":
                        head_rms(*task[1:])
                    elif kind == "base_a":
                        pool.wait_ge(xn_ready, FG * f + FG)
                        link(POOL.tensor_tensor(xs[:, fs], xs[:, fs], xn[:, fs], ALU.add))
                    elif kind == "base_b":
                        if f == 0:
                            pool.wait_ge(vec_in, 16)
                        POOL.tensor_tensor(xs[:, fs], xs[:, fs], every(V_BO), ALU.add).then_inc(base_ready, 1)
                    elif kind == "ffn_b":
                        pool.wait_ge(normed2, f + 1)
                        link(POOL.tensor_tensor(xf[:, fs], xf[:, fs], every(V_GAMMA), ALU.mult))
                    elif kind == "ffn_shift":
                        POOL.tensor_tensor(xf[:, fs], xf[:, fs], every(V_BETA), ALU.add).then_inc(xf_ready, 1)
                    elif kind == "ffn_c":
                        pool.wait_ge(signs_ready, f + 1)
                        slopes = ss[:].rearrange("p (o t) j -> p o (t j)", o=1).broadcast_to([P, FG, C])
                        POOL.tensor_tensor(big[:], big[:], slopes, ALU.mult).then_inc(signed, 1)
                    elif kind == "ffn_pick":
                        pool.wait_ge(choice_ready, f + 1)
                        POOL.tensor_tensor(big[:].rearrange("p n (t j) -> p (n t) j", j=SLICE),
                                           xf[:, fs].rearrange("p n (t j) -> p (n t) j", j=SLICE),
                                           chosen[:, fs].rearrange("p n (t o) -> p (n t) o", o=1)
                                           .broadcast_to([P, FG * TILES, SLICE]), ALU.mult).then_inc(slice_ready, 1)
                    elif kind == "pick":
                        pool.wait_ge(delta_ready, PICKS.index(f) + 1)
                        if PICKS.index(f):
                            pool.wait_ge(delta_added, PICKS.index(f))
                        for i in range(FG):
                            ob = chosen[:, FG * f + i].rearrange("p (t o) -> p t o", o=1).broadcast_to([P, TILES, SLICE])
                            db = delta[:, i:i + 1].broadcast_to([P, TILES, SLICE])
                            last = POOL.tensor_tensor(big[:, i].rearrange("p (t j) -> p t j", j=SLICE), ob, db, ALU.mult)
                        link(last)
                    elif kind == "pick_add":
                        if f not in EARLY_F:
                            pool.wait_ge(read, use(("out_project", FG * f + FG - 1)) + 1)
                        POOL.tensor_tensor(xs[:, fs], xs[:, fs], big[:], ALU.add).then_inc(delta_added, 1)

        @block.scalar
        def _(act):
            act.dma_start(idn[:], ident).then_inc(ident_in, 16)
            act.dma_start(wn[:], wnorm).then_inc(wn_in, 16)
            act.dma_start(tab_raw[:], tables).then_inc(tab_in, 16)
            act.dma_start(vec[:], vectors).then_inc(vec_in, 16)
            act.dma_start(rows[:], grid_rows).then_inc(rows_in, 16)
            act.dma_start(wo_sb[:], wo).then_inc(wo_in, 16)
            nc.scalar.preload_act_table(ACT.Tanh)
            act.wait_ge(const_ready, 3)
            for t in range(EARLY):
                act.wait_ge(early_filled, t + 1)
                bank = scores[:, R * t:R * t + R].rearrange("p r q -> p (r q)")
                nc.scalar.copy(raw[:, t], bank[:, 0:QKW])
                if t % 2 == 0 and t:
                    act.wait_ge(ssq_ready, t // 2)
                ins = nc.scalar.activation(sq[:, t % 2], bank[:, 0:QKW], ACT.Square)
                if t % 2:
                    ins.then_inc(sq_ready, 1)
                nc.scalar.copy(val[:, t, :, 0:D], bank[:, QKW:PROJ].rearrange("p (g d) -> p g d", g=G))
                nc.scalar.copy(val_low[HALF:P, t, :, 0:D], bank[HALF:P, PROJ:PROJ + G * D].rearrange("p (g d) -> p g d", g=G))\
                    .then_inc(early_read, 1)
            act.wait_ge(first_parts, 1)
            for h0, h1, places in LAYS[0]:
                count = len(range(SLOTS)[places])
                v = parts[:, 0, 0, D * h0:D * h1].rearrange("p (h o d) -> p h o d", o=1, d=D)
                last = nc.scalar.copy(combos[:, 0, h0:h1, places], v.broadcast_to([P, h1 - h0, count, D]))
            last.then_inc(lay_done, 1)
            act.wait_ge(crossed, 1)
            nc.scalar.copy(qT[:, 0, 0:H // 2], cross_q[0][:, 0:P * H // 2].rearrange("p (h q) -> p h q", q=P)).then_inc(cross_read_act, 1)
            for u in range(NU + 1):
                if u < NU:
                    act.wait_ge(scores_ready, u + 1)
                    if u >= PRING:
                        act.wait_ge(pv_done, u - PRING + 1)
                    nc.scalar.activation(used(probs[:, u % PRING], u), used(scores[:], u), ACT.Tanh, scale=SCORE_SCALE)\
                        .then_inc(tanh_done, 1)
                if u:
                    pr = used(probs[:, (u - 1) % PRING], u - 1)
                    act.wait_ge(tanh_done, u)
                    nc.scalar.activation(pr, pr, ACT.Exp, scale=SOFT_CAP).then_inc(exp_done, 1)

        @block.tensor
        def _(pe):
            def take(task):
                n = use(task)
                if n >= 2:
                    pe.wait_ge(read, n - 1)
                if n in (2, 3):
                    pe.wait_ge(cross_read_dve, CROSSED)
                return banks[n % 2]

            def after(task):
                pe.wait_ge(read, use(task) + 1)

            def score(u):
                s, kb = UNITS[u]
                kt = s - s % TB + kb
                if u == 0:
                    pe.wait_ge(cross_read_act, 1)
                if u == FIRST[s] and s < CROSSED:
                    pe.wait_ge(cross_read_dve, s + 1)
                elif u == FIRST[s]:
                    pe.wait_ge(turned, 32 * (s - CROSSED + 1))
                if u:
                    pe.wait_ge(tanh_done, u)
                if kb < s % TB:
                    for g in range(G):
                        last = nc.tensor.matmul(scores[:, R * g:R * g + R, :], kT[:, kt, g, :],
                                                qT[:, s % QRING, R * g:R * g + R, :], start=True, stop=True)
                else:
                    hi, lo = packed(scores[:])
                    for g in range(G):
                        q = qT[:, s % QRING, R * g:R * g + R]
                        nc.tensor.matmul(hi[:, g], kT[:, kt, g, :], q[:, :, HALF:P], start=True, stop=True)
                        for k in range(2):
                            last = nc.tensor.matmul(lo[HALF * k:HALF * k + HALF, g], kT[:, kt, g, 0:HALF],
                                                    q[:, R // 2 * k:R // 2 * k + R // 2, 0:HALF], start=True, stop=True)
                last.then_inc(scores_ready, 1)

            def value(u):
                s, kb = UNITS[u]
                kt = s - s % TB + kb
                pe.wait_ge(exp_done, u + 1)
                if kb == s % TB:
                    pe.wait_ge(mask_done, s + 1)
                if u == FIRST[s] and s >= 2:
                    pe.wait_ge(oacc_read, s - 1)
                if u == 0:
                    pe.wait_ge(cross_read_dve, CROSSED)
                    pe.wait_ge(const_ready, 4)
                projected(pe, kt)
                hi, lo = packed(probs[:, u % PRING])
                for g in range(G):
                    for r in range(R):
                        acc = oacc[VW * r:VW * r + VW, s % 2, P * g:P * g + P]
                        if kb < s % TB:
                            last = nc.tensor.matmul(acc, val[:, kt, g, :], probs[:, u % PRING, R * g + r, :],
                                                    start=False, stop=(u == LAST[s]), skip_group_check=True)
                        else:
                            nc.tensor.matmul(acc[:, HALF:P], val[:, kt, g, :], hi[:, g, r],
                                             start=(g == 0), stop=(u == LAST[s]), skip_group_check=True)
                if kb == s % TB:
                    for g in range(G):
                        for r in range(R):
                            k = r // (R // 2)
                            part = slice(HALF * k, HALF * k + HALF)
                            v = val_low[part, kt, g, :] if k else val[part, kt, g, :]
                            last = nc.tensor.matmul(oacc[VW * r:VW * r + VW, s % 2, P * g:P * g + HALF],
                                                    v, lo[part, g, r % (R // 2)],
                                                    start=False, stop=(u == LAST[s]), skip_group_check=True)
                last.then_inc(pv_done, 1)

            def stay_warm(n):
                for _ in range(n):
                    nc.tensor.matmul(banks[1][:, 0:P], masked[:], masked[:], start=True, stop=True)

            def do(task):
                kind = task[0]
                if kind == "turn":
                    t, n = task[1:]
                    bank = take(task)
                    pe.wait_ge(xn_ready, t + n)
                    if t == 0:
                        pe.wait_ge(ident_in, 16)
                    for i in range(n):
                        for c in range(2):
                            o = P * (2 * i + c)
                            last = nc.tensor.transpose(bank[:, o:o + P], xn[:, t + i, P * c:P * c + P], idn[:])
                    last.then_inc(filled, 1)
                elif kind == "signs":
                    bank = take(task)
                    pe.wait_ge(signs_rhs, 1)
                    pe.wait_ge(const_ready, 2)
                    nc.tensor.matmul(bank[:, 0:C], ones[:], sdiag[:].rearrange("k t j -> k (t j)"),
                                     start=True, stop=True).then_inc(filled, 1)
                elif kind == "project_a":
                    t = task[1]
                    bank = take(("project", t))
                    after(("turn", t - t % 2, 2))
                    nc.tensor.matmul(bank[:, 0:PROJ], xnT[:, t % 2, 0], wproj_sb[:, 0], start=True, stop=False)
                elif kind == "project":
                    t = task[1]
                    if t < EARLY:
                        bank = scores[:, R * t:R * t + R].rearrange("p r q -> p (r q)")
                        after(("turn", t - t % 2, 2))
                        if t == 0:
                            pe.wait_ge(wproj_in, 16)
                        nc.tensor.matmul(bank[:, 0:PROJ], xnT[:, t % 2, 0], wproj_sb[:, 0], start=True, stop=False)
                    else:
                        bank = banks[use(task) % 2]
                    nc.tensor.matmul(bank[:, 0:PROJ], xnT[:, t % 2, 1], wproj_sb[:, 1], start=False, stop=True)
                    for c in range(2):
                        last = nc.tensor.matmul(bank[HALF:P, PROJ:PROJ + G * D], xnT[:, t % 2, c, 0:HALF], wproj_sb[:, c, QKW:PROJ],
                                                start=(c == 0), stop=(c == 1), skip_group_check=True)
                    last.then_inc(early_filled if t < EARLY else filled, 1)
                elif kind == "cross":
                    t = task[1]
                    if t == 0:
                        stay_warm(REWARM)
                        pe.wait_ge(early_read, EARLY)
                        pe.wait_ge(idb_ready, 1)
                        pe.wait_ge(lay_done, 1)
                    pe.wait_ge(combos_ready, t + 1)
                    for h in range(HG):
                        dst, o = (cross_q[t], P * h) if h < H else (cross_k[t], P * (h - H))
                        last = nc.tensor.transpose(dst[:, o:o + P], combos[:, t, h].rearrange("p s d -> p (s d)"), idb[:])
                    last.then_inc(crossed, 1)
                elif kind == "suffix":
                    b = task[1]
                    bank = take(task)
                    pe.wait_ge(sums_ready, b + 1)
                    qts = SUFFIX[task[2]]
                    q0, q1 = qts[0], min(qts[-1] + 1, TB - 1)

                    def columns(n):
                        return bank[:, 0:n * G * (D + 1)].rearrange("p (q g d) -> p q g d", q=n, g=G)

                    nc.tensor.matmul(columns(len(qts)), masked_high[:], val[:, TB * b + q0:TB * b + q0 + len(qts), :, 0:D + 1],
                                     start=True, stop=False, skip_group_check=True)
                    last = nc.tensor.matmul(columns(q1 - q0), masked[:], suffix[:, b, q0:q1], start=False, stop=True,
                                            skip_group_check=True)
                    last.then_inc(filled, 1)
                elif kind == "out_norm":
                    s = task[1]
                    bank = take(task)
                    pe.wait_ge(oacc_read, s + 1)
                    for g in range(G):
                        last = nc.tensor.transpose(bank[:, P * g:P * g + P], oT[:, s % ORING, P * g:P * g + P], idn[:])
                    last.then_inc(filled, 1)
                elif kind == "out_turn":
                    bank = take(task)
                    pe.wait_ge(y_ready, task[1] + 1)
                    for c in range(2):
                        last = nc.tensor.transpose(bank[:, P * c:P * c + P], y[:, P * c:P * c + P], idn[:])
                    last.then_inc(filled, 1)
                elif kind == "out_project":
                    if task[1] == 0:
                        pe.wait_ge(wo_in, 16)
                    bank = take(task)
                    after(("out_turn", task[1]))
                    for c in range(2):
                        last = nc.tensor.matmul(bank[:, 0:C], yT[:, c], wo_sb[:, c], start=(c == 0), stop=(c == 1))
                    last.then_inc(filled, 1)
                elif kind == "extremes":
                    bank = take(task)
                    pe.wait_ge(lowb_ready, 1)
                    nc.tensor.transpose(bank[:, 0:P], low[:].rearrange("p a t -> p (a t)"), idn[:]).then_inc(filled, 1)
                elif kind == "extremes_row":
                    bank = take(task)
                    after(("extremes",))
                    nc.tensor.matmul(bank[:, 0:P], lowb[:], idn[:], start=True, stop=True).then_inc(filled, 1)
                elif kind == "pick_turn":
                    f = task[1]
                    bank = take(task)
                    for i in range(FG):
                        last = nc.tensor.transpose(bank[0:TILES, P * i:P * i + P], chosen[:, FG * f + i, :], idn[:])
                    last.then_inc(filled, 1)
                elif kind == "pick":
                    bank = take(task)
                    after(("pick_turn", task[1]))
                    for i in range(FG):
                        last = nc.tensor.matmul(bank[:, P * i:P * i + P], chT[:, i], rows[:, 0:P], start=True, stop=True)
                    last.then_inc(filled, 1)

            pe.wait_ge(const_ready, 1)
            stay_warm(WARM)
            for u in range(-1, NU + LAG):
                if 0 <= u < NU:
                    score(u)
                if u >= LAG:
                    value(u - LAG)
                for task in PLAN.get(u, ()):
                    do(task)

        @block.vector
        def _(dve):
            chain = [0]

            def link(ins):
                chain[0] += 1
                ins.then_inc(dve_chain, 1)
                dve.wait_ge(dve_chain, chain[0])

            V = nc.vector

            def rsqrt(v, n):
                g0, a, b = (newton_v[:, j, 0:n] for j in range(3))
                link(V.tensor_scalar(g0.bitcast(i32), v.bitcast(i32), -0.5, RSQRT_MAGIC, ALU.mult, ALU.add))
                for _ in range(3):
                    link(V.tensor_tensor(a, v, g0, ALU.mult))
                    link(V.scalar_tensor_tensor(b, a, -0.5, g0, ALU.mult, ALU.mult))
                    link(V.scalar_tensor_tensor(g0, b, 1.5, g0, ALU.add, ALU.mult))
                return g0

            def moments(src, t0, n, k):
                if k > MVRING:
                    dve.wait_ge(rstd_ready, k - MVRING)
                if k:
                    dve.wait_ge(stats_ready, k)
                for i in range(n):
                    last = V.bn_stats(stats[:, i], src[:, t0 + i])
                link(last)
                for i in range(n):
                    last = V.bn_aggr(mv[:, k % MVRING, i], stats[:, i])
                last.then_inc(stats_ready, 1)

            def center(src, dst, t0, n, k):
                if k:
                    dve.wait_ge(rstd_ready, k)
                for i in range(n):
                    yield V.tensor_scalar(dst[:, t0 + i], src[:, t0 + i], mv[:, k % MVRING, i, 0:1],
                                          rstd[:, k % MVRING, i:i + 1], ALU.subtract, ALU.mult)

            def rope_a(t0, n):
                k, m, half = ROPES.index(("rope_a", t0, n)), n * HG, D // 2
                heads = raw[:, t0 % RAW:t0 % RAW + n].rearrange("p n (h d) -> p n h d", d=D)
                tv = tmp[:, k % 2, 0:n].rearrange("p n (h d) -> p n h d", d=D)
                projected(dve, t0 + n - 1)
                for w, (h0, h1) in enumerate(((0, H), (H, HG))):
                    for lo, hi in ((0, half), (half, D)):
                        sin = tab[:, t0 % TB:t0 % TB + n, 1, w:w + 1, lo:hi].broadcast_to([P, n, h1 - h0, half])
                        last = V.tensor_tensor(tv[:, :, h0:h1, lo:hi], heads[:, :, h0:h1, D - hi:D - lo], sin, ALU.mult)
                last.then_inc(sin_ready, 1)
                dve.wait_ge(sq_ready, k + 1)
                V.tensor_reduce(ssq[:, k % 2, 0:m], sq[:, 0:n].rearrange("p n (h d) -> p (n h) d", d=D), X, ALU.add)\
                    .then_inc(ssq_ready, 1)
                if k == 0:
                    dve.wait_ge(ssq_ready, 1)
                    mean, r = newton_v[:, 3, 0:m], rms[:, 0, 0:m]
                    link(V.tensor_scalar(mean, ssq[:, 0, 0:m], 1.0 / D, None, ALU.mult))
                    g0 = rsqrt(mean, m)
                    link(V.tensor_tensor(r, mean, g0, ALU.mult))
                    link(V.tensor_scalar(r, r, RMS_EPS, None, ALU.add))

            def group(t0):
                k = next(k for k, (_, a, n) in enumerate(ROPES) if a <= t0 < a + n)
                return k, t0 - ROPES[k][1]

            def lay(t0, n, j, done=None):
                for i in range(n):
                    c = combos[:, (t0 + i) % 2]
                    for h0, h1, places in LAYS[j]:
                        count = len(range(SLOTS)[places])
                        v = parts[:, j, group(t0)[1] + i, D * h0:D * h1].rearrange("p (h o d) -> p h o d", o=1, d=D)
                        last = V.tensor_copy(c[:, h0:h1, places], v.broadcast_to([P, h1 - h0, count, D]))
                    if done is not None:
                        last.then_inc(done, 1)

            def rope_b(t0, n):
                k, o = group(t0)
                m = n * HG
                dve.wait_ge(sin_ready, k + 1)
                dve.wait_ge(cos_ready, k + 1)
                V.tensor_tensor(rot[:, k % 2, o:o + n], rot[:, k % 2, o:o + n], tmp[:, k % 2, o:o + n], ALU.add).then_inc(dve_chain, 1)
                chain[0] += 1
                if k:
                    dve.wait_ge(rms_ready, k)
                inv, rr = ssq[:, k % 2, HG * o:HG * o + m], rot[:, k % 2, o:o + n]
                link(V.reciprocal(inv, rms[:, k % 2, HG * o:HG * o + m]))
                rall = rr.rearrange("p n (h d) -> p (n h) d", d=D)
                link(V.tensor_tensor(rall, rall, inv.rearrange("p (h o) -> p h o", o=1).broadcast_to([P, m, D]), ALU.mult))

            def rope_split(t0, n):
                k, o = group(t0)
                rr, p1 = rot[:, k % 2, o:o + n], parts[:, 0, o:o + n]
                if t0 == CROSSED:
                    dve.wait_ge(lay_done, 1)
                V.tensor_copy(p1, rr).then_inc(first_parts, 1)
                dve.wait_ge(first_parts, SPLITS.index(("rope_split", t0, n)) + 1)
                V.tensor_tensor(rr, rr, p1, ALU.subtract).then_inc(dve_chain, 1)
                chain[0] += 1
                if t0 + n > CROSSED + 2:
                    dve.wait_ge(turned, 32 * (t0 + n - 2 - CROSSED))
                elif t0 >= CROSSED:
                    dve.wait_ge(crossed, t0 + n - 2)
                if t0:
                    lay(t0, n, 0)

            def rope_c(t0, n):
                k, o = group(t0)
                rr, p2, p3 = rot[:, k % 2, o:o + n], parts[:, 1, o:o + n], parts[:, 2, o:o + n]
                dve.wait_ge(dve_chain, chain[0])
                link(V.tensor_copy(p2, rr))
                V.tensor_tensor(p3, rr, p2, ALU.subtract).then_inc(dve_chain, 1)
                chain[0] += 1
                lay(t0, n, 1)

            def rope_d(t0, n):
                dve.wait_ge(dve_chain, chain[0])
                lay(t0, n, 2, combos_ready)

            def ffn_choose(f):
                fs = slice(FG * f, FG * f + FG)
                dve.wait_ge(signed, f + 1)
                link(V.tensor_reduce(tsc[:].rearrange("p n t -> p (n t)"), big[:].rearrange("p n (t j) -> p (n t) j", j=SLICE), X, ALU.add))
                link(V.tensor_reduce(csc[:], tsc[:].rearrange("p n (c k) -> p (n c) k", k=PER), X, ALU.add))

            def ffn_pick(f):
                fs = slice(FG * f, FG * f + FG)
                kc = vec[:, V_KEY:V_KEY + TILES].rearrange("p (o t) -> p o t", o=1).broadcast_to([P, FG, TILES])
                link(V.scalar_tensor_tensor(key[:], tsc[:], float(PER), kc, ALU.mult, ALU.add))
                k3 = key[:].rearrange("p n (c k) -> p (n c) k", k=PER)
                cb = csc[:].rearrange("p (c o) -> p c o", o=1).broadcast_to([P, FG * CLUSTERS, PER])
                link(V.scalar_tensor_tensor(k3, cb, float(PER * P), k3, ALU.mult, ALU.add))
                link(V.tensor_reduce(best[:], key[:], X, ALU.max))
                bb = best[:].rearrange("p (n o) -> p n o", o=1).broadcast_to([P, FG, TILES])
                V.tensor_tensor(chosen[:, fs], key[:], bb, ALU.is_equal).then_inc(choice_ready, 1)

            def ffn_extremes(f):
                fs = slice(FG * f, FG * f + FG)
                dve.wait_ge(slice_ready, f + 1)
                link(V.tensor_reduce(xsl[:, fs], big[:].rearrange("p n (t j) -> p n j t", j=SLICE), X, ALU.add))
                V.tensor_reduce(ends[:, 0], xsl[:, fs], X, ALU.min)
                link(V.tensor_reduce(ends[:, 1], xsl[:, fs], X, ALU.max))
                link(V.tensor_scalar(ends[:, 1], ends[:, 1], -1.0, None, ALU.mult))

            def ffn_cand(f):
                oh = chosen[:, FG * f:FG * f + FG]
                for a in range(2):
                    eb = ends[:, a].rearrange("p (n o) -> p n o", o=1).broadcast_to([P, FG, TILES])
                    V.tensor_tensor(cand[:, a], oh, eb, ALU.mult)
                link(V.tensor_scalar(key[:], oh, -BIG, BIG, ALU.mult, ALU.add))
                for a in range(2):
                    last = V.tensor_tensor(cand[:, a], cand[:, a], key[:], ALU.add)
                link(last)

            def ffn_least(f):
                least = low if f == 0 else key
                for a in range(2):
                    last = V.tensor_reduce(least[:, a], cand[:, a].rearrange("p n t -> p t n"), X, ALU.min)
                link(last)
                if f:
                    ins = V.tensor_tensor(low[:], low[:], key[:, 0:2], ALU.min)
                    if f == NF - 1:
                        ins.then_inc(lowb_ready, 1)
                    else:
                        link(ins)

            def do(task):
                kind = task[0]
                if task in USES:
                    bank = banks[use(task) % 2]
                    dve.wait_ge(filled, use(task) + 1)
                if kind == "norm_a":
                    t0, n = task[1:]
                    for i, (c0, cn) in enumerate(xchunks):
                        if c0 < t0 + n and t0 < c0 + cn:
                            dve.wait_ge(x_in[i], 16)
                    k = STATS.index(task)
                    moments(xs, t0, n, k)
                    if k == 0:
                        dve.wait_ge(stats_ready, 1)
                        link(V.tensor_scalar(newton_v[:, 3, 0:n], mv[:, 0, 0:n, 1], LN_EPS, None, ALU.add))
                        link(V.tensor_copy(rstd[:, 0, 0:n], rsqrt(newton_v[:, 3, 0:n], n)))
                elif kind == "norm_b":
                    t0, n = task[1:]
                    for ins in center(xs, xn, t0, n, STATS.index(("norm_a", t0, n))):
                        ins.then_inc(xn_ready, 1)
                elif kind == "turn":
                    n = task[2]
                    V.tensor_copy(xnT[:, task[1] % 2:task[1] % 2 + n].rearrange("p i c t -> p (i c t)"), bank[:, 0:C * n]).then_inc(read, 1)
                elif kind == "project":
                    t = task[1]
                    if t < EARLY:
                        return
                    if t == EARLY:
                        dve.wait_ge(const_ready, 3)
                    if t >= RAW:
                        dve.wait_ge(cos_ready, next(k for k, (_, t0, n) in enumerate(ROPES) if t0 + n > t - RAW) + 1)
                    V.tensor_copy(val[:, t, :, 0:D], bank[:, QKW:PROJ].rearrange("p (g d) -> p g d", g=G))
                    V.tensor_copy(val_low[HALF:P, t, :, 0:D], bank[HALF:P, PROJ:PROJ + G * D].rearrange("p (g d) -> p g d", g=G))
                    V.tensor_copy(raw[:, t % RAW], bank[:, 0:QKW]).then_inc(read, 1)
                    dve.wait_ge(read, use(task) + 1)
                elif kind == "tables":
                    dve.wait_ge(ident_in, 16)
                    V.tensor_copy(idb[:], idn[:]).then_inc(idb_ready, 1)
                    dve.wait_ge(wn_in, 16)
                    dve.wait_ge(tab_in, 16)
                    for k in range(2):
                        for w in range(2):
                            last = V.tensor_tensor(tab[:, :, k, w], tab_raw[:, :, k], wn[:, k, w:w + 1].broadcast_to([P, TB, D]), ALU.mult)
                    last.then_inc(tab_ready, 1)
                elif kind == "slopes":
                    dve.wait_ge(rows_in, 16)
                    half = SLICE * GRID
                    link(V.tensor_reduce(sgn[:], rows[:, half:2 * half].rearrange("k (j g) -> k j g", g=GRID), X, ALU.add))
                    link(V.tensor_scalar(sgn[:], sgn[:], 1.0 / GRID, None, ALU.mult))
                    link(V.tensor_scalar(sgn_ge[:], sgn[:], 0.0, -1.0, ALU.is_ge, ALU.add))
                    link(V.scalar_tensor_tensor(sgn[:], sgn[:], 0.0, sgn_ge[:], ALU.is_gt, ALU.add))
                    dve.wait_ge(ident_in, 16)
                    V.tensor_tensor(sdiag[:], idn[0:TILES, 0:TILES].rearrange("k (t o) -> k t o", o=1).broadcast_to([TILES, TILES, SLICE]),
                                    sgn[:].rearrange("k (o j) -> k o j", o=1).broadcast_to([TILES, TILES, SLICE]), ALU.mult).then_inc(signs_rhs, 1)
                    link(V.tensor_scalar(rows[:, 0:2 * half], rows[:, 0:2 * half], rows[:, 2 * half:2 * half + 1], None, ALU.mult))
                elif kind == "cross":
                    t = task[1]
                    dve.wait_ge(crossed, t + 1)
                    h0 = H // 2 if t == 0 else 0
                    V.tensor_copy(qT[:, t, h0:H], cross_q[t][:, P * h0:P * H].rearrange("p (h q) -> p h q", q=P))
                    V.tensor_copy(kT[:, t], cross_k[t].rearrange("p (h q) -> p h q", q=P)).then_inc(cross_read_dve, 1)
                elif kind == "rope_a":
                    rope_a(*task[1:])
                elif kind == "rope_b":
                    rope_b(*task[1:])
                elif kind == "rope_split":
                    rope_split(*task[1:])
                elif kind == "rope_c":
                    rope_c(*task[1:])
                elif kind == "rope_d":
                    rope_d(*task[1:])
                elif kind == "signs":
                    V.tensor_copy(ss[:].rearrange("p t j -> p (t j)"), bank[:, 0:C]).then_inc(read, 1)
                elif kind == "suffix":
                    qts = SUFFIX[task[2]]
                    V.tensor_copy(suffix[:, task[1], qts[0]:qts[-1] + 1].rearrange("p q g d -> p (q g d)"),
                                  bank[:, 0:len(qts) * G * (D + 1)]).then_inc(read, 1)
                elif kind == "drain":
                    s = task[1]
                    dve.wait_ge(pv_done, LAST[s] + 1)
                    if s >= ORING:
                        dve.wait_ge(filled, use(("out_norm", s - ORING)) + 1)
                    V.tensor_copy(oT[:, s % ORING], oacc[:, s % 2]).then_inc(oacc_read, 1)
                elif kind == "out_norm":
                    s = task[1]
                    b, qt = divmod(s, TB)
                    acc = bank[:].rearrange("p (g r w) -> p g r w", g=G, w=VW)
                    dst = osum[:].rearrange("p (g r) d -> p g r d", g=G)
                    if s:
                        dve.wait_ge(y_ready, s)
                    k = next(k for k, qts in enumerate(SUFFIX) if qt in qts)
                    dve.wait_ge(read, use(("suffix", b, k)) + 1)
                    sfx = suffix[:, b, qt].rearrange("p g (o d) -> p g o d", o=1).broadcast_to([P, G, R, D + 1])
                    V.tensor_tensor(dst, acc[:, :, :, 0:D + 1], sfx, ALU.add).then_inc(read, 1)
                    dve.wait_ge(read, use(task) + 1)
                    link(V.reciprocal(oinv[:], osum[:, :, D]))
                    ob = oinv[:].rearrange("p (h o) -> p h o", o=1).broadcast_to([P, H, D])
                    V.tensor_tensor(y[:].rearrange("p (h d) -> p h d", d=D), osum[:, :, 0:D], ob, ALU.mult).then_inc(y_ready, 1)
                elif kind == "out_turn":
                    V.tensor_copy(yT[:].rearrange("p c t -> p (c t)"), bank[:, 0:C]).then_inc(read, 1)
                elif kind == "out_project":
                    s = task[1]
                    dve.wait_ge(base_ready, s // FG + 1)
                    if s // FG in EARLY_F:
                        dve.wait_ge(delta_added, PICKS.index(s // FG) + 1)
                    V.tensor_tensor(xs[:, s], xs[:, s], bank[:, 0:C], ALU.add).then_inc(read, 1)
                elif kind == "ffn_a":
                    f = task[1]
                    moments(xn, FG * f, FG, STATS.index(task))
                elif kind == "ffn_b":
                    f = task[1]
                    dve.wait_ge(base_ready, f + 1)
                    tile = next(t for t in USES if t[0] == "turn" and t[1] + t[2] == FG * f + FG)
                    dve.wait_ge(filled, use(tile) + 1)
                    for i, ins in enumerate(center(xn, xf, FG * f, FG, STATS.index(("ffn_a", f)))):
                        if i == FG - 1:
                            ins.then_inc(normed2, 1)
                elif kind == "ffn_c":
                    f = task[1]
                    fs = slice(FG * f, FG * f + FG)
                    dve.wait_ge(xf_ready, f + 1)
                    link(V.tensor_scalar(big[:], xf[:, fs], 0.0, -1.0, ALU.is_ge, ALU.add))
                    V.scalar_tensor_tensor(big[:], xf[:, fs], 0.0, big[:], ALU.is_gt, ALU.add).then_inc(signs_ready, 1)
                elif kind == "ffn_d":
                    ffn_choose(task[1])
                elif kind == "ffn_e":
                    ffn_extremes(task[1])
                elif kind == "ffn_pick":
                    ffn_pick(task[1])
                elif kind == "ffn_cand":
                    ffn_cand(task[1])
                elif kind == "ffn_least":
                    ffn_least(task[1])
                elif kind == "extremes":
                    link(V.tensor_reduce(lowc[:], bank[:, 0:P], X, ALU.min))
                    V.tensor_scalar(lowb[:], masked[:], 0.0, lowc[:], ALU.mult, ALU.add).then_inc(read, 1)
                elif kind == "extremes_row":
                    V.tensor_copy(lowr[:].rearrange("p a t -> p (a t)"), bank[:, 0:P]).then_inc(read, 1)
                    dve.wait_ge(read, use(task) + 1)
                elif kind == "grid_a":
                    wide = big[:].rearrange("p a c -> p (a c)").rearrange("p (n t) -> p n t", n=NT)
                    for a in range(2):
                        lb = lowr[:, a:a + 1].broadcast_to([P, NT, TILES])
                        link(V.tensor_tensor(wide, chosen[:], lb, ALU.mult))
                        link(V.tensor_reduce(tmn[:, a], wide, X, ALU.add))
                    link(V.scalar_tensor_tensor(rng[:], tmn[:, 1], -1.0, tmn[:, 0], ALU.mult, ALU.subtract))
                    link(V.tensor_scalar(rng[:], rng[:], 1e-8, None, ALU.add))
                    link(V.reciprocal(rng[:], rng[:]))
                elif kind == "grid_b":
                    mb = tmn[:, 0].rearrange("p (n o) -> p n o", o=1).broadcast_to([P, NT, SLICE])
                    rb = rng[:].rearrange("p (n o) -> p n o", o=1).broadcast_to([P, NT, SLICE])
                    link(V.tensor_tensor(u16[:], xsl[:], mb, ALU.subtract))
                    link(V.tensor_tensor(u16[:], u16[:], rb, ALU.mult))
                    link(V.tensor_scalar(u16[:], u16[:], 0.0, UMAX, ALU.max, ALU.min))
                    link(V.tensor_scalar(u16[:], u16[:], float(GRID), None, ALU.mult))
                elif kind == "grid_c":
                    flat = u16[:].rearrange("p n j -> p (n j)")
                    ub = flat.rearrange("p (m o) -> p m o", o=1).broadcast_to([P, NT * SLICE, GRID])
                    gb = vec[:, V_GRID:V_GRID + GRID].rearrange("p (o g) -> p o g", o=1).broadcast_to([P, NT * SLICE, GRID])
                    hv = hot.rearrange("p n (j g) -> p (n j) g", g=GRID)
                    giv = gi[:].rearrange("p n j -> p (n j)")
                    link(V.tensor_tensor(hv, ub, gb, ALU.is_ge))
                    link(V.tensor_reduce(giv, hv[:, :, 1:GRID], X, ALU.add))
                    ib = giv.rearrange("p (m o) -> p m o", o=1).broadcast_to([P, NT * SLICE, GRID])
                    link(V.tensor_tensor(hv, ib, gb, ALU.is_equal))
                    link(V.tensor_tensor(flat, flat, giv, ALU.subtract))
                elif kind == "pick_turn":
                    V.tensor_copy(chT[:].rearrange("k n t -> k (n t)"), bank[0:TILES, :]).then_inc(read, 1)
                elif kind == "pick":
                    f = task[1]
                    fs = slice(FG * f, FG * f + FG)
                    picked = hot[:, fs]
                    if PICKS.index(f):
                        dve.wait_ge(delta_added, PICKS.index(f))
                    for a in range(2):
                        last = V.tensor_tensor(bprod[:, :, a], bank[:].rearrange("p (n a m) -> p n a m", n=FG, a=2)[:, :, a],
                                               picked, ALU.mult)
                    last.then_inc(read, 1)
                    dve.wait_ge(read, use(task) + 1)
                    link(V.tensor_reduce(bsel[:].rearrange("p n a j -> p (n a j)"),
                                         bprod.rearrange("p n a (j g) -> p (n a j) g", g=GRID), X, ALU.add))
                    link(V.tensor_tensor(delta[:], bsel[:, :, 1], u16[:, fs], ALU.mult))
                    V.tensor_tensor(delta[:], delta[:], bsel[:, :, 0], ALU.add).then_inc(delta_ready, 1)

            for u in range(-1, NU + LAG):
                for task in PLAN.get(u, ()):
                    do(task)


def kernel(**inputs):
    import concourse.bacc as bacc
    from concourse.bass_utils import run_bass_kernel_spmd

    a = {k: np.asarray(v) for k, v in inputs.items()}

    def tiled(w, n):
        return np.ascontiguousarray(w.reshape(n, P, -1).transpose(1, 0, 2))

    wproj = tiled(np.concatenate([a["L0_attn_Wq"], a["L0_attn_Wk"], a["L0_attn_Wv"]], 0).T, 2)
    tile_no = np.arange(TILES)
    tie = -(P * (tile_no // PER) + tile_no % PER).astype(np.float32)
    vectors = np.concatenate([a["L0_ffn_ln_gamma"], a["L0_ffn_ln_beta"], a["L0_attn_bo"], tie,
                              np.arange(GRID, dtype=np.float32)])
    inv_freq = (1.0 / 10000.0 ** (np.arange(0, D, 2, dtype=np.float32) / np.float32(D))).astype(np.float32)
    freqs = np.outer(np.arange(T, dtype=np.float32), inv_freq).astype(np.float32)
    cos, sin = np.cos(freqs), np.sin(freqs)
    tables = np.stack([np.concatenate([cos, cos], 1), np.concatenate([sin, -sin], 1)], 1)
    qw, kw = a["L0_attn_q_norm_w"], a["L0_attn_k_norm_w"]
    half = D // 2
    wnorm = np.stack([qw, kw, np.concatenate([qw[half:], qw[:half]]), np.concatenate([kw[half:], kw[:half]])])
    arrays = {
        "x": tiled(a["L0_attn_x"].reshape(NTOK, C), NT),
        "wproj": wproj,
        "wo": tiled(a["L0_attn_Wo"].T, 2),
        "vectors": np.ascontiguousarray(np.broadcast_to(vectors, (P, V_ALL))),
        "tables": np.ascontiguousarray(tables.reshape(TB, P, 2, D).transpose(1, 0, 2, 3)),
        "wnorm": np.ascontiguousarray(np.broadcast_to(wnorm.reshape(1, 2, 2, D), (P, 2, 2, D))),
        "grid_rows": np.ascontiguousarray(np.concatenate([
            a["L0_ffn_spline_bases"].reshape(TILES, -1), a["L0_ffn_spline_slopes"].reshape(TILES, -1),
            a["L0_ffn_output_scale"].reshape(TILES, 1)], 1)),
        "ident": np.eye(P, dtype=np.float32),
    }
    nc = bacc.Bacc("TRN2", target_bir_lowering=False, num_devices=1)
    args = [nc.dram_tensor(k, v.shape, mybir.dt.from_np(v.dtype), kind="ExternalInput").ap() for k, v in arrays.items()]
    out = nc.dram_tensor("out", (P, NT, C), mybir.dt.float32, kind="ExternalOutput").ap()
    build(nc, *args, out)
    r = run_bass_kernel_spmd(nc, [arrays], core_ids=[0])
    o = np.asarray(r.results[0]["out"])
    return np.ascontiguousarray(o.transpose(1, 0, 2)).reshape(B, T, C)
```
